# Optimizing a Trainium2 kernel written in Bass

```python
import numpy as np
import jax
import jax.numpy as jnp

def _softmax(x, axis=-1):
    return jax.nn.softmax(x, axis=axis)

def _gelu(x):
    return jax.nn.gelu(x, approximate=True)

def _silu(x):
    return jax.nn.silu(x)

def _sigmoid(x):
    return jax.nn.sigmoid(x)

def _layernorm(x, axis=-1, eps=1e-05):
    m = jnp.mean(x, axis=axis, keepdims=True)
    v = jnp.var(x, axis=axis, keepdims=True)
    return (x - m) / jnp.sqrt(v + eps)

def _scatter_add(tgt, idx, src, axis=0):
    return tgt.at[idx].add(src)

def _segment_sum(src, seg, n):
    return jax.ops.segment_sum(src, seg, n)
kernel_name = 'mk_perceiver_d1_seqx_r8_023289'

def setup_inputs(seed: int=0):
    np.random.seed(seed)
    _w = jnp.asarray

    def _rec_inputs():
        import jax
        import jax.numpy as jnp
        _rk = jax.random.key(seed)
        x = -0.0002928 + 1 * jax.random.normal(jax.random.fold_in(_rk, 1), (8, 64, 512), jnp.float32)
        _lenS = 64 - jax.random.randint(jax.random.fold_in(_rk, 7), (8,), 0, max(1, 64 // 4) + 1, jnp.int32)
        _lenS2 = 1601 - jax.random.randint(jax.random.fold_in(_rk, 8), (8,), 0, max(1, 1601 // 4) + 1, jnp.int32)
        _ctx_4096P = jax.random.normal(jax.random.fold_in(_rk, 11), (8, 16, 512), jnp.float32)
        _ctx_4096c = jax.random.dirichlet(jax.random.fold_in(_rk, 511), 0.3 * jnp.ones((16,), jnp.float32), (8, 1601))
        _ctx_4096t = jnp.einsum('bsk,bkd->bsd', _ctx_4096c, _ctx_4096P)
        _ctx_4096t = _ctx_4096t * jax.lax.rsqrt(jnp.mean(jnp.square(_ctx_4096t)) + 1e-12) * 0.953939
        ctx_4096 = -2.8382e-05 + 0.999851 * (_ctx_4096t + 0.3 * jax.random.normal(jax.random.fold_in(_rk, 611), (8, 1601, 512), jnp.float32))
        _validS = jnp.arange(64)[None, :] < _lenS[:, None]
        _validS2 = jnp.arange(1601)[None, :] < _lenS2[:, None]
        _causal = jnp.tril(jnp.ones((64, 64), dtype=bool))
        mask_1x1xSxS2_ff0 = jnp.where(jnp.ones((1, 1, 64, 1601), dtype=bool), 0.0, -1000000000.0).astype(jnp.float32)
        return (x, ctx_4096, mask_1x1xSxS2_ff0)
    x, ctx_4096, mask_1x1xSxS2_ff0 = _rec_inputs()

    def _L0_xattn_setup():
        import jax, jax.numpy as jnp
        import numpy as np
        NUM_HEADS = 32
        NUM_KV_HEADS = 8
        HEAD_DIM = 128
        HIDDEN = 512
        EPS = 1e-05

        def rmsnorm(x, w, eps=EPS):
            xf = x.astype(jnp.float32)
            var = jnp.mean(xf * xf, axis=-1, keepdims=True)
            return w * (xf * jax.lax.rsqrt(var + eps)).astype(x.dtype)
        key = jax.random.key(seed)
        ks = jax.random.split(key, 10)
        B, Q, KV = (1, 128, 6404)
        s = 1.0 / np.sqrt(HIDDEN)
        return {'hidden_states': jax.random.normal(ks[0], (B, Q, HIDDEN), jnp.float32), 'cross_attention_states': jax.random.normal(ks[1], (B, KV, HIDDEN), jnp.float32), 'attention_mask': jnp.zeros((B, 1, Q, KV), jnp.float32), 'q_proj_w': jax.random.normal(ks[2], (NUM_HEADS * HEAD_DIM, HIDDEN), jnp.float32) * s, 'k_proj_w': jax.random.normal(ks[3], (NUM_KV_HEADS * HEAD_DIM, HIDDEN), jnp.float32) * s, 'v_proj_w': jax.random.normal(ks[4], (NUM_KV_HEADS * HEAD_DIM, HIDDEN), jnp.float32) * s, 'o_proj_w': jax.random.normal(ks[5], (HIDDEN, NUM_HEADS * HEAD_DIM), jnp.float32) * s, 'q_norm_w': jnp.ones((HEAD_DIM,), jnp.float32), 'k_norm_w': jnp.ones((HEAD_DIM,), jnp.float32)}
    _L0_xattn_all = _L0_xattn_setup()
    _L0_xattn_in = {k: v for k, v in _L0_xattn_all.items() if k in ('q_proj_w', 'k_proj_w', 'v_proj_w', 'o_proj_w', 'q_norm_w', 'k_norm_w')}
    del _L0_xattn_all

    def _L0_attn_setup():
        import jax, jax.numpy as jnp
        import numpy as np
        from jax import lax
        H = 64
        P = 64
        N = 128
        G = 8
        K = 4
        D_MODEL = 512
        I = H * P
        GN = G * N
        CONV_DIM = I + 2 * GN
        PROJ = I + CONV_DIM + H
        EPS = 1e-05
        GROUP_SIZE = I // G

        def _reference_tuple_inner(hidden_states, in_proj_w, conv_weight, conv_bias, dt_bias, A_log, D, norm_weight, out_proj_w):
            B, L, _ = hidden_states.shape
            proj = jnp.einsum('bld,pd->blp', hidden_states, in_proj_w)
            gate = proj[..., :I]
            hbc = proj[..., I:I + CONV_DIM]
            dt = proj[..., -H:]
            pad = jnp.pad(hbc, ((0, 0), (K - 1, 0), (0, 0)))
            conv = conv_bias
            for k in range(K):
                conv = conv + pad[:, k:k + L, :] * conv_weight[:, k]
            xBC = jax.nn.silu(conv)
            x = xBC[..., :I].reshape(B, L, H, P)
            Bm = xBC[..., I:I + GN].reshape(B, L, G, N)
            Cm = xBC[..., I + GN:].reshape(B, L, G, N)
            hpg = H // G
            B_h = jnp.repeat(Bm, hpg, axis=2)
            C_h = jnp.repeat(Cm, hpg, axis=2)
            dt_p = jax.nn.softplus(dt + dt_bias)
            A = -jnp.exp(A_log)
            dA = jnp.exp(dt_p * A)
            dtx = dt_p[..., None] * x

            def step(state, inp):
                dA_t, dtx_t, B_t, C_t = inp
                state = state * dA_t[..., None, None] + dtx_t[..., None] * B_t[:, :, None, :]
                y_t = jnp.einsum('bhpn,bhn->bhp', state, C_t)
                return (state, y_t)
            xs = (jnp.moveaxis(dA, 1, 0), jnp.moveaxis(dtx, 1, 0), jnp.moveaxis(B_h, 1, 0), jnp.moveaxis(C_h, 1, 0))
            state0 = jnp.zeros((B, H, P, N), jnp.float32)
            final_state, ys = lax.scan(step, state0, xs)
            y = jnp.moveaxis(ys, 0, 1) + x * D[None, None, :, None]
            y = y.reshape(B, L, I)
            yg = y.reshape(B, L, G, GROUP_SIZE)
            var = jnp.mean(yg * yg, axis=-1, keepdims=True)
            yn = (yg * lax.rsqrt(var + EPS)).reshape(B, L, I) * norm_weight
            yn = yn * jax.nn.silu(gate)
            out = jnp.einsum('bli,di->bld', yn, out_proj_w)
            conv_state_new = jnp.moveaxis(hbc[:, L - (K - 1):, :], 1, 2)
            return (out, conv_state_new, final_state)
        key = jax.random.key(seed)
        ks = jax.random.split(key, 6)
        B, L = (2, 256)
        s = 0.02
        return {'hidden_states': jax.random.normal(ks[0], (B, L, D_MODEL), jnp.float32), 'in_proj_w': jax.random.normal(ks[1], (PROJ, D_MODEL), jnp.float32) * s, 'conv_weight': jax.random.normal(ks[2], (CONV_DIM, K), jnp.float32) * s, 'conv_bias': jnp.zeros((CONV_DIM,), jnp.float32), 'dt_bias': jnp.ones((H,), jnp.float32), 'A_log': jnp.log(jnp.arange(1, H + 1, dtype=jnp.float32)), 'D': jnp.ones((H,), jnp.float32), 'norm_weight': jnp.ones((I,), jnp.float32), 'out_proj_w': jax.random.normal(ks[3], (D_MODEL, I), jnp.float32) * s}
    _L0_attn_all = _L0_attn_setup()
    _L0_attn_in = {k: v for k, v in _L0_attn_all.items() if k in ('in_proj_w', 'conv_weight', 'conv_bias', 'dt_bias', 'A_log', 'D', 'norm_weight', 'out_proj_w')}
    del _L0_attn_all

    def _L0_ffn_setup():
        import jax, jax.numpy as jnp
        import numpy as np
        R = 16
        LORA_ALPHA = 16
        SCALING = LORA_ALPHA / R
        key = jax.random.key(seed)
        kx, kr, ka = jax.random.split(key, 3)
        B, S, D, DO, E = (4, 256, 512, 512, 8)
        x = jax.random.normal(kx, (B, S, D), dtype=jnp.float32)
        bound_r = 1.0 / np.sqrt(D)
        route_w = jax.random.uniform(kr, (E, D), jnp.float32, -bound_r, bound_r)
        bound_a = 1.0 / np.sqrt(D)
        A = jax.random.uniform(ka, (E, R, D), jnp.float32, -bound_a, bound_a)
        kb = jax.random.fold_in(key, 7)
        Bw = jax.random.normal(kb, (E, DO, R), dtype=jnp.float32) * 0.02
        return {'x': x, 'route_w': route_w, 'A': A, 'Bw': Bw}
    _L0_ffn_all = _L0_ffn_setup()
    _L0_ffn_in = {k: v for k, v in _L0_ffn_all.items() if k in ('route_w', 'A', 'Bw')}
    del _L0_ffn_all
    return {'x': x, 'ctx_4096': ctx_4096, 'mask_1x1xSxS2_ff0': mask_1x1xSxS2_ff0, 'L0_xattn_q_proj_w': _L0_xattn_in['q_proj_w'], 'L0_xattn_k_proj_w': _L0_xattn_in['k_proj_w'], 'L0_xattn_v_proj_w': _L0_xattn_in['v_proj_w'], 'L0_xattn_o_proj_w': _L0_xattn_in['o_proj_w'], 'L0_xattn_q_norm_w': _L0_xattn_in['q_norm_w'], 'L0_xattn_k_norm_w': _L0_xattn_in['k_norm_w'], 'L0_attn_in_proj_w': _L0_attn_in['in_proj_w'], 'L0_attn_conv_weight': _L0_attn_in['conv_weight'], 'L0_attn_conv_bias': _L0_attn_in['conv_bias'], 'L0_attn_dt_bias': _L0_attn_in['dt_bias'], 'L0_attn_A_log': _L0_attn_in['A_log'], 'L0_attn_D': _L0_attn_in['D'], 'L0_attn_norm_weight': _L0_attn_in['norm_weight'], 'L0_attn_out_proj_w': _L0_attn_in['out_proj_w'], 'L0_ffn_route_w': _L0_ffn_in['route_w'], 'L0_ffn_A': _L0_ffn_in['A'], 'L0_ffn_Bw': _L0_ffn_in['Bw']}

def reference(x, ctx_4096, mask_1x1xSxS2_ff0, L0_xattn_q_proj_w, L0_xattn_k_proj_w, L0_xattn_v_proj_w, L0_xattn_o_proj_w, L0_xattn_q_norm_w, L0_xattn_k_norm_w, L0_attn_in_proj_w, L0_attn_conv_weight, L0_attn_conv_bias, L0_attn_dt_bias, L0_attn_A_log, L0_attn_D, L0_attn_norm_weight, L0_attn_out_proj_w, L0_ffn_route_w, L0_ffn_A, L0_ffn_Bw):
    import jax
    import jax.numpy as jnp

    def _L0_xattn_ref(hidden_states, cross_attention_states, attention_mask, q_proj_w, k_proj_w, v_proj_w, o_proj_w, q_norm_w, k_norm_w):
        import jax, jax.numpy as jnp
        import numpy as np
        NUM_HEADS = 32
        NUM_KV_HEADS = 8
        HEAD_DIM = 128
        HIDDEN = 512
        EPS = 1e-05

        def rmsnorm(x, w, eps=EPS):
            xf = x.astype(jnp.float32)
            var = jnp.mean(xf * xf, axis=-1, keepdims=True)
            return w * (xf * jax.lax.rsqrt(var + eps)).astype(x.dtype)
        B, Q, _ = hidden_states.shape
        KV = cross_attention_states.shape[1]
        n_rep = NUM_HEADS // NUM_KV_HEADS
        q = (hidden_states @ q_proj_w.T).reshape(B, Q, NUM_HEADS, HEAD_DIM).transpose(0, 2, 1, 3)
        k = (cross_attention_states @ k_proj_w.T).reshape(B, KV, NUM_KV_HEADS, HEAD_DIM).transpose(0, 2, 1, 3)
        v = (cross_attention_states @ v_proj_w.T).reshape(B, KV, NUM_KV_HEADS, HEAD_DIM).transpose(0, 2, 1, 3)
        q = rmsnorm(q, q_norm_w)
        k = jnp.repeat(k, n_rep, axis=1)
        v = jnp.repeat(v, n_rep, axis=1)
        k = rmsnorm(k, k_norm_w)
        scale = 1.0 / np.sqrt(HEAD_DIM)
        scores = jnp.einsum('bhqd,bhkd->bhqk', q, k) * scale + attention_mask
        attn = jax.nn.softmax(scores.astype(jnp.float32), axis=-1).astype(q.dtype)
        out = jnp.einsum('bhqk,bhkd->bhqd', attn, v)
        out = out.transpose(0, 2, 1, 3).reshape(B, Q, NUM_HEADS * HEAD_DIM)
        return out @ o_proj_w.T

    def _L0_attn_ref(hidden_states, in_proj_w, conv_weight, conv_bias, dt_bias, A_log, D, norm_weight, out_proj_w):
        import jax, jax.numpy as jnp
        import numpy as np
        from jax import lax
        H = 64
        P = 64
        N = 128
        G = 8
        K = 4
        D_MODEL = 512
        I = H * P
        GN = G * N
        CONV_DIM = I + 2 * GN
        PROJ = I + CONV_DIM + H
        EPS = 1e-05
        GROUP_SIZE = I // G

        def _reference_tuple_inner(hidden_states, in_proj_w, conv_weight, conv_bias, dt_bias, A_log, D, norm_weight, out_proj_w):
            B, L, _ = hidden_states.shape
            proj = jnp.einsum('bld,pd->blp', hidden_states, in_proj_w)
            gate = proj[..., :I]
            hbc = proj[..., I:I + CONV_DIM]
            dt = proj[..., -H:]
            pad = jnp.pad(hbc, ((0, 0), (K - 1, 0), (0, 0)))
            conv = conv_bias
            for k in range(K):
                conv = conv + pad[:, k:k + L, :] * conv_weight[:, k]
            xBC = jax.nn.silu(conv)
            x = xBC[..., :I].reshape(B, L, H, P)
            Bm = xBC[..., I:I + GN].reshape(B, L, G, N)
            Cm = xBC[..., I + GN:].reshape(B, L, G, N)
            hpg = H // G
            B_h = jnp.repeat(Bm, hpg, axis=2)
            C_h = jnp.repeat(Cm, hpg, axis=2)
            dt_p = jax.nn.softplus(dt + dt_bias)
            A = -jnp.exp(A_log)
            dA = jnp.exp(dt_p * A)
            dtx = dt_p[..., None] * x

            def step(state, inp):
                dA_t, dtx_t, B_t, C_t = inp
                state = state * dA_t[..., None, None] + dtx_t[..., None] * B_t[:, :, None, :]
                y_t = jnp.einsum('bhpn,bhn->bhp', state, C_t)
                return (state, y_t)
            xs = (jnp.moveaxis(dA, 1, 0), jnp.moveaxis(dtx, 1, 0), jnp.moveaxis(B_h, 1, 0), jnp.moveaxis(C_h, 1, 0))
            state0 = jnp.zeros((B, H, P, N), jnp.float32)
            final_state, ys = lax.scan(step, state0, xs)
            y = jnp.moveaxis(ys, 0, 1) + x * D[None, None, :, None]
            y = y.reshape(B, L, I)
            yg = y.reshape(B, L, G, GROUP_SIZE)
            var = jnp.mean(yg * yg, axis=-1, keepdims=True)
            yn = (yg * lax.rsqrt(var + EPS)).reshape(B, L, I) * norm_weight
            yn = yn * jax.nn.silu(gate)
            out = jnp.einsum('bli,di->bld', yn, out_proj_w)
            conv_state_new = jnp.moveaxis(hbc[:, L - (K - 1):, :], 1, 2)
            return (out, conv_state_new, final_state)
        return _reference_tuple_inner(hidden_states, in_proj_w, conv_weight, conv_bias, dt_bias, A_log, D, norm_weight, out_proj_w)[0]

    def _L0_ffn_ref(x, route_w, A, Bw):
        import jax, jax.numpy as jnp
        import numpy as np
        R = 16
        LORA_ALPHA = 16
        SCALING = LORA_ALPHA / R
        logits = jnp.einsum('bsd,ed->bse', x, route_w)
        topk_v, topk_idx = jax.lax.top_k(logits, 1)
        E = logits.shape[-1]
        route_weight = jax.nn.one_hot(topk_idx[..., 0], E, dtype=logits.dtype) * topk_v
        h = jnp.einsum('bsd,erd->bser', x, A)
        wh = route_weight[..., None] * h
        out = jnp.einsum('bser,eor->bso', wh, Bw) * SCALING
        return out
    x = x + _L0_xattn_ref(_layernorm(x, axis=-1), ctx_4096, mask_1x1xSxS2_ff0, L0_xattn_q_proj_w, L0_xattn_k_proj_w, L0_xattn_v_proj_w, L0_xattn_o_proj_w, L0_xattn_q_norm_w, L0_xattn_k_norm_w)
    x = x + _L0_attn_ref(_layernorm(x, axis=-1), L0_attn_in_proj_w, L0_attn_conv_weight, L0_attn_conv_bias, L0_attn_dt_bias, L0_attn_A_log, L0_attn_D, L0_attn_norm_weight, L0_attn_out_proj_w)
    x = x + _L0_ffn_ref(_layernorm(x, axis=-1), L0_ffn_route_w, L0_ffn_A, L0_ffn_Bw)
    return x

_drawn_inputs = setup_inputs


def setup_inputs(seed=0):
    import zlib

    import numpy as np

    out = dict(_drawn_inputs(seed))
    spreads = {'L0_xattn_q_norm_w': (1.0, 0.2),
     'L0_xattn_k_norm_w': (1.0, 0.2),
     'L0_attn_conv_bias': (0.0, 0.1),
     'L0_attn_dt_bias': (1.0, 0.6),
     'L0_attn_D': (1.0, 0.535),
     'L0_attn_norm_weight': (1.0, 0.2)}
    factors = {'L0_attn_A_log': 8.0}
    for name, (base, spread) in spreads.items():
        noise = np.random.default_rng([zlib.crc32(name.encode()), seed]).standard_normal(out[name].shape)
        drawn = base * np.exp(spread * noise) if base else spread * noise
        out[name] = jnp.asarray(drawn.astype(out[name].dtype))
    for name, factor in factors.items():
        out[name] = (out[name] * factor).astype(out[name].dtype)
    return out
```

```python
import concourse.bass as bass
from concourse import mybir
from contextlib import ExitStack

F32 = mybir.dt.float32
F16 = mybir.dt.float16
ALU = mybir.AluOpType
ACT = mybir.ActivationFunctionType
AX = mybir.AxisListType

P = 128
BATCH, TOK, HID = 8, 64, 512
KEYS = 1601
KC = HID // P
HEADS, KV_HEADS, HD = 32, 8, 128
REP = HEADS // KV_HEADS
QC = REP * TOK
KT = -(-KEYS // P)
TAIL = KEYS - (KT - 1) * P
KPAD = KT * P
CH = [(0, 400), (400, 400), (800, 400), (1200, KEYS - 1200)]
NCH = len(CH)
EPS = 1e-5
NEG = -3.0e38

S_CTX, S_W = 16.0, 64.0
S_Q = 64.0
S_KV = 16.0
S_SQ = 2.0
P_LN = 6.931471805599453


STEP_ORDER = ["S0 S1 K0 S2 S3 K1 N S4 V0 S5 K2 S6 M K3 V1 D V2 V3",
              "S0 S1 K0 S2 S3 K1 N S4 V0 S5 K2 S6 M K3 V1 C0 D V2 C1 V3",
              "S0 C2 S1 K0 S2 C3 N S3 K1 S4 S5 K2 S6 M K3 V0 D V1 V2",
              "S0 S1 S2 S3 S4 S5 S6 N M D"]


def wait(eng, sem, value):
    if isinstance(value, int) and value <= 0:
        return
    eng.wait_ge(sem, value)


def row(ap, i):
    if isinstance(i, int):
        return ap[i]
    return ap[bass.ds(i, 1)].rearrange("o p n -> (o p) n")


def cross_attention(nc, ctxT, maskT, kv_parts, ctx_parts, q_hi, q_lo, q_stored, o_dram, NB=BATCH):
    with ExitStack() as ctx:
        def sb(name, shape, dt):
            return ctx.enter_context(nc.sbuf_tensor(name, shape, dt))

        def pb(name, shape):
            return ctx.enter_context(nc.psum_tensor(name, shape, F32))

        def sem(name):
            return ctx.enter_context(nc.semaphore(name))

        U = KV_HEADS
        ctx_f, ctx_h, ctx_l = ctx_parts
        w_h, w_l = kv_parts
        k_h = sb("k_h", [P, 2, KPAD], F16)
        k_l = sb("k_l", [P, 2, KPAD], F16)
        sq_f = sb("sq_f", [P, 2, CH[-1][1] + 3], F32)
        sq_h = sb("sq_h", [P, KPAD], F16)
        sq_l = sb("sq_l", [P, KPAD], F16)
        v_h = sb("v_h", [P, 2, KT, 2 * HD], F16)
        v_l = sb("v_l", [P, 2, KT, 2 * HD], F16)
        S = sb("S", [P, 2, KT, QC], F32)
        p_h = sb("p_h", [P, 2, KT, QC], F16)
        p_l = sb("p_l", [P, 2, KT, QC], F16)
        mask = sb("mask", [P, KT, TOK], F32)
        qh = sb("qh", [P, U, QC], F16)
        ql = sb("ql", [P, U, QC], F16)
        o_st = sb("o_st", [P, U, QC], F32)
        mx = sb("mx", [P, QC], F32)
        mb = sb("mb", [P, QC], F32)
        psum_p = sb("psum_p", [P, 2, QC], F32)
        z = sb("z", [P, 2, 16], F32)
        rk = sb("rk", [P, 2, 16], F32)
        half = sb("half", [P, 16], F32)
        lnb = sb("lnb", [P, 1], F32)
        ones = sb("ones", [P, P], F32)
        one_h = sb("one_h", [P, 1], F16)

        pF = [pb(f"pF{i}", [P, 512]) for i in range(3)]
        pS = [pb(f"pS{i}", [P, 2, QC]) for i in range(2)]
        pO = [pb(f"pO{i}", [P, 2, QC]) for i in range(2)]
        pQ = pb("pQ", [P, 16])

        consts = sem("consts")
        mask_in = sem("mask_in")
        ctx_in = [sem(f"ctx_in{n}") for n in range(NCH)]
        ctx_hi = sem("ctx_hi")
        ctx_lo = sem("ctx_lo")
        q_in = [sem(f"q_in{s}") for s in range(U)]
        proj = sem("proj")
        fill_hi = sem("fill_hi")
        fill_lo = sem("fill_lo")
        sqh_ok = sem("sqh_ok")
        sql_ok = sem("sql_ok")
        ss_ok = sem("ss_ok")
        z_ok = sem("z_ok")
        rk_ok = sem("rk_ok")
        s_ok = sem("s_ok")
        s_out = sem("s_out")
        mx_ok = sem("mx_ok")
        mb_ok = sem("mb_ok")
        turn = sem("turn")
        sub_ok = sem("sub_ok")
        ex_ok = sem("ex_ok")
        ph_ok = sem("ph_ok")
        pl_ok = sem("pl_ok")
        tree = sem("tree")
        sum_ok = sem("sum_ok")
        pv_ok = sem("pv_ok")
        den_ok = sem("den_ok")
        rec_ok = sem("rec_ok")
        o_ok = sem("o_ok")
        o_stored = [sem(f"o_stored{h}") for h in range(2)]

        HALF = [(0, 7), (7, KT)]

        VF = -(-KT // 2)

        def v_fills(s):
            return list(range(3, VF)) if s % 2 == 0 else [0, 1, 2]

        def order(s, last):
            vs = v_fills(s)
            text = STEP_ORDER[0 if s < U - 2 else 1 if s == U - 2 and not last else 0 if s < U - 1 else 3 if last else 2]
            seq = []
            for item in text.split():
                i = int(item[1:] or 0)
                if item[0] != "V":
                    seq.append((item[0], i))
                elif i < len(vs):
                    seq.append(("V", vs[i]))
            return seq

        PRO = [("K", n) for n in range(NCH)] + [("V", f) for f in (0, 1, 2)]
        FILLS = U * NCH + U // 2 * VF

        number = {("K", 0, n): n for n in range(NCH)}
        number |= {("V", 0, f): NCH + f for f in (0, 1, 2)}
        at = len(PRO)
        for s in range(U):
            for kind, i in order(s, False):
                if kind == "K":
                    number["K", s + 1, i] = at
                elif kind == "V":
                    number["V", (s + 1) // 2, i] = at
                else:
                    continue
                at += 1
        assert at == len(PRO) + FILLS

        chunk_used = [1 + max(number["K", U - 1, i], number["V", U // 2 - 1, (c0 + w - 1) // (2 * P)])
                      for i, (c0, w) in enumerate(CH)]

        def fill_no(b, kind, job, i):
            return FILLS * b + number[kind, job, i]

        def loop(eng, body):
            body(0)
            if NB > 2:
                with eng.Fori(1, NB - 1) as b:
                    body(b)
            if NB > 1:
                body(NB - 1)

        def before(b, s, n):
            if s >= n:
                return b, s - n
            return None if isinstance(b, int) and b == 0 else (b - 1, s - n + U)

        def is_last(b):
            return isinstance(b, int) and b == NB - 1

        block = ctx.enter_context(nc.Block())

        @block.sync
        def _(sp):
            sp.wait_ge(consts, 8)
            sp.dma_start(mask[:, 0:KT - 1, :], maskT[0:(KT - 1) * P, :].rearrange("(t p) q -> p t q", p=P)).then_inc(mask_in, 16)
            sp.dma_start(mask[0:TAIL, KT - 1, :], maskT[(KT - 1) * P:KEYS, :]).then_inc(mask_in, 16)

            def load_ctx(b, n):
                c0, w = CH[n]
                src = row(ctxT, b)[:, c0:c0 + w].rearrange("(k p) c -> p k c", p=P)
                sp.dma_start(ctx_f[:, :, c0:c0 + w], src).then_inc(ctx_in[n], 16)

            def load_q(b, s):
                cols = slice(s * QC, (s + 1) * QC)
                sp.dma_start(qh[:, s, :], row(q_hi, b)[:, cols]).then_inc(q_in[s], 16)
                sp.dma_start(ql[:, s, :], row(q_lo, b)[:, cols]).then_inc(q_in[s], 16)

            for i in range(2):
                sp.wait_ge(q_stored[i], 32 * HEADS // 8)
            for s in range(U):
                load_q(0, s)

            def store_o(b, h, after):
                sp.wait_ge(o_ok, after)
                c = slice(h * U // 2 * QC, (h + 1) * U // 2 * QC)
                sp.dma_start(row(o_dram, b)[:, c], o_st[:, 4 * h:4 * h + 4, :].rearrange("p u q -> p (u q)")).then_inc(o_stored[h], 16)

            def body(b):
                last = is_last(b)
                if not last:
                    wait(sp, ctx_lo, NCH * b)
                    for n in range(NCH):
                        load_ctx(b + 1, n)
                for s in range(U):
                    if s == 2 and not (isinstance(b, int) and b == 0):
                        store_o(b - 1, 1, U * b)
                    if s == 6:
                        store_o(b, 0, U * b + 4)
                    if not last:
                        wait(sp, s_ok, 7 * (U * b + s + 1))
                        load_q(b + 1, s)
            loop(sp, body)
            store_o(NB - 1, 1, U * NB)
            for h in range(2):
                sp.wait_ge(o_stored[h], 16 * NB)

        @block.tensor
        def _(pe):
            pe.wait_ge(consts, 8)

            def split3(out, a, b, cols, first, final):
                for j, (x, y) in enumerate(((a[0], b[0]), (a[0], b[1]), (a[1], b[0]))):
                    mm = pe.matmul(out, x, y, start=first and j == 0, stop=final and j == 2)
                return mm

            def fill(b, kind, job, i):
                n = fill_no(b, kind, job, i)
                wait(pe, fill_lo, n - 2)
                bank = pF[number[kind, job, i] % 3]
                if kind == "K":
                    head = job % U
                    nb = b + job // U
                    c0, w = CH[i]
                    wait(pe, ctx_lo, NCH * (nb - 1) + i + 1)
                    for k in range(KC):
                        cols = slice(head * HD, (head + 1) * HD)
                        mm = split3(bank[:, 0:w],
                                    (w_h[:, 0, k, cols], w_l[:, 0, k, cols]),
                                    (ctx_h[:, k, c0:c0 + w], ctx_l[:, k, c0:c0 + w]), w, k == 0, k == KC - 1)
                else:
                    pair = job % (U // 2)
                    if job in (0, U // 2) and i == 0:
                        wait(pe, ctx_lo, NCH * (b + job // (U // 2)))
                    cols = slice(pair * 2 * HD, (pair + 1) * 2 * HD)
                    for t in range(2 * i, min(2 * i + 2, KT)):
                        m = min(P, KEYS - t * P)
                        for k in range(KC):
                            mm = split3(bank[0:m, (t % 2) * 256:(t % 2) * 256 + 256],
                                        (ctx_h[:, k, t * P:t * P + m], ctx_l[:, k, t * P:t * P + m]),
                                        (w_h[:, 1, k, cols], w_l[:, 1, k, cols]), 256, k == 0, k == KC - 1)
                mm.then_inc(proj, 1)

            def scores(b, s, p):
                u = U * b + s
                m = 7 * u + p
                wait(pe, s_out, m - 1)
                if p == 0:
                    wait(pe, fill_lo, fill_no(b, "K", s, NCH - 1) + 1)
                    wait(pe, q_in[s], 32 * (b + 1))
                bank = pS[(s * 7 + p) % 2]
                for t in range(2 * p, min(2 * p + 2, KT)):
                    kk = slice(t * P, (t + 1) * P)
                    mm = split3(bank[:, t % 2, :], (k_h[:, s % 2, kk], k_l[:, s % 2, kk]),
                                (qh[:, s, :], ql[:, s, :]), QC, True, True)
                mm.then_inc(s_ok, 1)

            def squares(b, s):
                u = U * b + s
                wait(pe, sqh_ok, NCH * (u + 1))
                wait(pe, sql_ok, NCH * (u + 1))
                wait(pe, z_ok, u)
                for t in range(KT):
                    kk = slice(t * P, (t + 1) * P)
                    pe.matmul(pQ[:, t:t + 1], sq_h[:, kk], one_h[:, :], start=True, stop=False)
                    mm = pe.matmul(pQ[:, t:t + 1], sq_l[:, kk], one_h[:, :], start=False, stop=True)
                mm.then_inc(ss_ok, 1)

            def values(b, s):
                u = U * b + s
                wait(pe, pl_ok, 2 * (u + 1))
                wait(pe, ph_ok, 2 * (u + 1))
                wait(pe, fill_lo, fill_no(b, "V", s // 2, VF - 1) + 1)
                wait(pe, o_ok, u - 1)
                bank = pO[s % 2]
                hv = slice((s % 2) * HD, (s % 2) * HD + HD)
                for t in range(KT):
                    mm = split3(bank[:, 0, :], (v_h[:, (s // 2) % 2, t, hv], v_l[:, (s // 2) % 2, t, hv]),
                                (p_h[:, s % 2, t, :], p_l[:, s % 2, t, :]), QC, t == 0, t == KT - 1)
                mm.then_inc(pv_ok, 1)

            def denominators(b, s):
                wait(pe, sum_ok, U * b + s + 1)
                pe.matmul(pO[s % 2][:, 1, :], ones[:, :], psum_p[:, s % 2, :], start=True, stop=True).then_inc(den_ok, 1)

            for kind, i in PRO:
                fill(0, kind, 0, i)
            squares(0, 0)

            def body(b):
                last = is_last(b)
                for s in range(U):
                    for kind, i in order(s, last):
                        if kind == "S":
                            scores(b, s, i)
                        elif kind == "K":
                            fill(b, kind, s + 1, i)
                        elif kind == "V":
                            fill(b, kind, (s + 1) // 2, i)
                        elif kind == "N" and before(b, s, 2):
                            denominators(*before(b, s, 2))
                    if not (last and s == U - 1):
                        squares(b, s + 1)
                    if s > 0:
                        values(b, s - 1)
                    elif not (isinstance(b, int) and b == 0):
                        values(b - 1, U - 1)
            loop(pe, body)
            denominators(NB - 1, U - 2)
            values(NB - 1, U - 1)
            denominators(NB - 1, U - 1)

        @block.scalar
        def _(act):
            def ctx_split(b, n):
                c0, w = CH[n]
                act.wait_ge(ctx_in[n], 16 * b)
                act.activation(ctx_h[:, :, c0:c0 + w], ctx_f[:, :, c0:c0 + w], ACT.Copy, scale=S_CTX).then_inc(ctx_hi, 1)

            def fill(b, kind, job, i):
                n = fill_no(b, kind, job, i)
                wait(act, proj, n + 1)
                bank = pF[number[kind, job, i] % 3]
                if kind == "K":
                    u = U * b + job
                    c0, w = CH[i]
                    c = NCH * u + i
                    if i == 0:
                        wait(act, s_ok, 7 * (u - 1))
                    act.activation(k_h[:, job % 2, c0:c0 + w], bank[:, 0:w], ACT.Copy, scale=S_KV / (S_CTX * S_W))
                    wait(act, sql_ok, c - 1)
                    act.activation(sq_f[:, i % 2, 0:w], bank[:, 0:w], ACT.Square, scale=S_SQ / (S_CTX * S_W)).then_inc(fill_hi, 1)
                    if i == 0:
                        wait(act, ss_ok, u)
                    act.wait_ge(fill_hi, n + 1)
                    act.activation(sq_h[:, c0:c0 + w], sq_f[:, i % 2, 0:w], ACT.Copy).then_inc(sqh_ok, 1)
                else:
                    if i == 0:
                        wait(act, pv_ok, U * b + 2 * job - 2)
                    tiles = min(2, KT - 2 * i)
                    m = P if tiles == 2 else TAIL
                    act.activation(v_h[0:m, job % 2, 2 * i:2 * i + tiles, :],
                                   bank[0:m, 0:256 * tiles].rearrange("p (t c) -> p t c", c=256),
                                   ACT.Copy, scale=S_KV / (S_CTX * S_W)).then_inc(fill_hi, 1)

            def probabilities(b, s, h):
                u = U * b + s
                t0, t1 = HALF[h]
                act.wait_ge(sub_ok, 2 * u + h + 1)
                act.activation(S[:, s % 2, t0:t1, :], S[:, s % 2, t0:t1, :], ACT.Exp, bias=lnb[:, 0:1]).then_inc(ex_ok, 1)
                wait(act, pv_ok, u - 1)
                act.wait_ge(ex_ok, 2 * u + h + 1)
                act.activation(p_h[:, s % 2, t0:t1, :], S[:, s % 2, t0:t1, :], ACT.Copy).then_inc(ph_ok, 1)

            act.wait_ge(consts, 8)
            for kind, i in PRO:
                fill(0, kind, 0, i)

            def body(b):
                last = is_last(b)
                first = isinstance(b, int) and b == 0
                for s in range(U):
                    prev = (b, s - 1) if s else (b - 1, U - 1)
                    if not (first and s == 0):
                        probabilities(*prev, 0)
                    done = first and s == 0
                    for kind, i in order(s, last):
                        if kind in "KV":
                            fill(b, kind, s + 1 if kind == "K" else (s + 1) // 2, i)
                            if not done:
                                probabilities(*prev, 1)
                                done = True
                        elif kind == "C":
                            wait(act, proj, FILLS * b + chunk_used[i])
                            ctx_split(b + 1, i)
                    if not done:
                        probabilities(*prev, 1)
            loop(act, body)
            for h in range(2):
                probabilities(NB - 1, U - 1, h)

        @block.vector
        def _(dve):
            dve.memset(k_h[:, :, KEYS:KPAD], 0.0).then_inc(consts, 1)
            dve.memset(k_l[:, :, KEYS:KPAD], 0.0).then_inc(consts, 1)
            dve.memset(sq_h[:, KEYS:KPAD], 0.0).then_inc(consts, 1)
            dve.memset(sq_l[:, KEYS:KPAD], 0.0).then_inc(consts, 1)
            dve.memset(one_h[:, :], 1.0)
            dve.memset(half[:, :], -0.5)
            dve.memset(lnb[:, :], P_LN)
            dve.memset(ones[:, :], 1.0).then_inc(consts, 1)
            dve.memset(mask[:, KT - 1, :], NEG).then_inc(consts, 1)
            dve.memset(v_h[:, :, KT - 1, :], 0.0).then_inc(consts, 1)
            dve.memset(v_l[:, :, KT - 1, :], 0.0).then_inc(consts, 1)
            def ctx_split(b, n):
                c0, w = CH[n]
                dve.wait_ge(ctx_hi, NCH * (b - 1) + n + 1)
                dve.scalar_tensor_tensor(out=ctx_l[:, :, c0:c0 + w], in0=ctx_f[:, :, c0:c0 + w], scalar=S_CTX,
                                         in1=ctx_h[:, :, c0:c0 + w], op0=ALU.mult, op1=ALU.subtract).then_inc(ctx_lo, 1)

            def fill(b, kind, job, i):
                n = fill_no(b, kind, job, i)
                dve.wait_ge(fill_hi, n + 1)
                bank = pF[number[kind, job, i] % 3]
                if kind == "K":
                    c0, w = CH[i]
                    c = NCH * (U * b + job) + i
                    dve.scalar_tensor_tensor(out=k_l[:, job % 2, c0:c0 + w], in0=bank[:, 0:w], scalar=S_KV / (S_CTX * S_W),
                                             in1=k_h[:, job % 2, c0:c0 + w], op0=ALU.mult, op1=ALU.subtract).then_inc(fill_lo, 1)
                    dve.wait_ge(sqh_ok, c + 1)
                    dve.tensor_tensor(sq_l[:, c0:c0 + w], sq_f[:, i % 2, 0:w], sq_h[:, c0:c0 + w], ALU.subtract).then_inc(sql_ok, 1)
                else:
                    tiles = min(2, KT - 2 * i)
                    m = P if tiles == 2 else TAIL
                    vv = v_h[0:m, job % 2, 2 * i:2 * i + tiles, :]
                    dve.scalar_tensor_tensor(out=v_l[0:m, job % 2, 2 * i:2 * i + tiles, :],
                                             in0=bank[0:m, 0:256 * tiles].rearrange("p (t c) -> p t c", c=256),
                                             scalar=S_KV / (S_CTX * S_W), in1=vv, op0=ALU.mult, op1=ALU.subtract).then_inc(fill_lo, 1)

            def norms(b, s):
                u = U * b + s
                wait(dve, ss_ok, u + 1)
                scale2 = (S_KV * S_Q) ** 2 * HD
                dve.tensor_scalar(z[:, s % 2, 0:KT], pQ[:, 0:KT], scale2 / (HD * S_SQ ** 2), scale2 * EPS,
                                  ALU.mult, ALU.add).then_inc(z_ok, 1)

            def evacuate(b, s, p):
                u = U * b + s
                if p == 0:
                    wait(dve, rk_ok, u + 1)
                    wait(dve, sum_ok, u - 1)
                wait(dve, s_ok, 7 * u + p + 1)
                bank = pS[(s * 7 + p) % 2]
                for t in range(2 * p, min(2 * p + 2, KT)):
                    ins = dve.scalar_tensor_tensor(
                        out=S[:, s % 2, t, :].rearrange("p (r q) -> p r q", r=REP),
                        in0=bank[:, t % 2, :].rearrange("p (r q) -> p r q", r=REP),
                        scalar=rk[:, s % 2, t:t + 1], in1=mask[:, t, :].unsqueeze(1).to_broadcast([P, REP, TOK]),
                        op0=ALU.mult, op1=ALU.add)
                ins.then_inc(s_out, 1)

            def maximum(b, s):
                u = U * b + s
                wait(dve, s_out, 7 * (u + 1))
                dve.tensor_reduce(mx[:, :], S[:, s % 2, :, :].rearrange("p t q -> p q t"), AX.X, ALU.max).then_inc(mx_ok, 1)

            def subtract(b, s, h):
                u = U * b + s
                if h == 0:
                    wait(dve, mb_ok, u + 1)
                t0, t1 = HALF[h]
                v = S[:, s % 2, t0:t1, :]
                dve.tensor_tensor(v, v, mb[:, :].unsqueeze(1).to_broadcast([P, t1 - t0, QC]), ALU.subtract).then_inc(sub_ok, 1)

            def output(b, s):
                u = U * b + s
                wait(dve, den_ok, u + 1)
                bank = pO[s % 2]
                if s % 4 == 0:
                    wait(dve, o_stored[s // 4], 16 * b)
                dve.reciprocal(o_st[:, s, :], bank[:, 1, :]).then_inc(rec_ok, 1)
                dve.wait_ge(rec_ok, u + 1)
                dve.scalar_tensor_tensor(out=o_st[:, s, :], in0=bank[:, 0, :], scalar=1.0 / S_KV, in1=o_st[:, s, :],
                                         op0=ALU.mult, op1=ALU.mult).then_inc(o_ok, 1)

            for kind, i in PRO:
                fill(0, kind, 0, i)
            norms(0, 0)
            dve.wait_ge(mask_in, 32)

            def body(b):
                last = is_last(b)
                first = isinstance(b, int) and b == 0
                for s in range(U):
                    for kind, i in order(s, last):
                        if kind == "S":
                            evacuate(b, s, i)
                        elif kind in "KV":
                            fill(b, kind, s + 1 if kind == "K" else (s + 1) // 2, i)
                        elif kind == "C":
                            ctx_split(b + 1, i)
                        elif kind == "M":
                            maximum(b, s)
                        elif kind == "D":
                            subtract(b, s, 0)
                            subtract(b, s, 1)
                        elif kind == "N" and before(b, s, 2):
                            output(*before(b, s, 2))
                    if not (last and s == U - 1):
                        norms(b, s + 1)
            loop(dve, body)
            output(NB - 1, U - 2)
            output(NB - 1, U - 1)

        @block.gpsimd
        def _(pool):
            def power(b, s):
                u = U * b + s
                wait(pool, z_ok, u + 1)
                wait(pool, s_out, 7 * (u - 1))
                pool.tensor_tensor(rk[:, s % 2, 0:KT], z[:, s % 2, 0:KT], half[:, 0:KT], ALU.pow).then_inc(rk_ok, 1)

            def reduce(b, s):
                u = U * b + s
                wait(pool, mx_ok, u + 1)
                pool.sem_inc(turn, 1)
                pool.partition_all_reduce(mb[:, :], mx[:, :], P, bass.bass_isa.ReduceOp.max).then_inc(mb_ok, 1)

            def low(b, s, h):
                u = U * b + s
                t0, t1 = HALF[h]
                wait(pool, ph_ok, 2 * u + h + 1)
                pool.tensor_tensor(p_l[:, s % 2, t0:t1, :], S[:, s % 2, t0:t1, :], p_h[:, s % 2, t0:t1, :],
                                   ALU.subtract).then_inc(pl_ok, 1)

            def total(b, s):
                u = U * b + s
                T = S[:, s % 2, :, :]
                wait(pool, pl_ok, 2 * (u + 1))
                pool.tensor_tensor(T[:, 0:6, :], T[:, 0:6, :], T[:, 6:12, :], ALU.add).then_inc(tree, 1)
                wait(pool, tree, 4 * u + 1)
                pool.tensor_tensor(T[:, 0:3, :], T[:, 0:3, :], T[:, 3:6, :], ALU.add).then_inc(tree, 1)
                wait(pool, tree, 4 * u + 2)
                pool.tensor_tensor(T[:, 0, :], T[:, 0, :], T[:, 1, :], ALU.add).then_inc(tree, 1)
                pool.tensor_tensor(T[:, 2, :], T[:, 2, :], T[:, 12, :], ALU.add).then_inc(tree, 1)
                wait(pool, tree, 4 * u + 4)
                wait(pool, den_ok, u - 1)
                pool.tensor_tensor(psum_p[:, s % 2, :], T[:, 0, :], T[:, 2, :], ALU.add).then_inc(sum_ok, 1)

            pool.wait_ge(consts, 8)
            power(0, 0)

            def body(b):
                last = is_last(b)
                first = isinstance(b, int) and b == 0
                for s in range(U):
                    prev = (b, s - 1) if s else (b - 1, U - 1)
                    have = not (first and s == 0)
                    if have:
                        low(*prev, 0)
                        low(*prev, 1)
                        total(*prev)
                    reduce(b, s)
                    if not (last and s == U - 1):
                        power(b, s + 1)
            loop(pool, body)
            low(NB - 1, U - 1, 0)
            low(NB - 1, U - 1, 1)
            total(NB - 1, U - 1)
S_H = 16.0
S_O = 64.0
S_Y = 16.0
GROUPS = 8
TT = BATCH * TOK // P
ND = BATCH * TOK
INNER = 4096
GCH = INNER // GROUPS // P
CONV = GCH + 2
TAPS = 4
SSM_HEADS, SSM_P = 64, 64
GH = SSM_HEADS // GROUPS
NPAR = CONV * TAPS + CONV + 2 * GCH
EXPERTS, RANK = 8, 16


def split3(pe, out, a, b, first, final):
    for j, (x, y) in enumerate(((a[0], b[0]), (a[0], b[1]), (a[1], b[0]))):
        mm = pe.matmul(out, x, y, start=first and j == 0, stop=final and j == 2)
    return mm


class LayerNorm:

    def __init__(self, nc, ctx, tag, x, ident, eps, banks, out):
        self.nc, self.x, self.ident, self.eps, self.banks, self.out = nc, x, ident, eps, banks, out
        self.st = ctx.enter_context(nc.sbuf_tensor(f"{tag}_st", [P, TT, 6], F32))
        self.mv = ctx.enter_context(nc.sbuf_tensor(f"{tag}_mv", [P, TT, 2], F32))
        self.sd = ctx.enter_context(nc.sbuf_tensor(f"{tag}_sd", [P, TT], F32))
        self.rs = ctx.enter_context(nc.sbuf_tensor(f"{tag}_rs", [P, TT], F32))
        self.xn = ctx.enter_context(nc.sbuf_tensor(f"{tag}_xn", [P, TT, HID], F32))
        self.moments, self.std, self.rstd, self.normed, self.turned, self.done = [
            ctx.enter_context(nc.semaphore(f"{tag}_{name}"))
            for name in "moments std rstd normed turned done".split()]
        if len(out) == 2:
            self.high = ctx.enter_context(nc.semaphore(f"{tag}_high"))

    def vector(self, dve):
        for t in range(TT):
            dve.bn_stats(self.st[:, t, :], self.x[:, t, :]).then_inc(self.moments, 1)
        for t in range(TT):
            dve.wait_ge(self.moments, TT)
            dve.bn_aggr(self.mv[:, t, :], self.st[:, t, :]).then_inc(self.moments, 1)
        dve.wait_ge(self.std, 1)
        dve.reciprocal(self.rs[:, :], self.sd[:, :]).then_inc(self.rstd, 1)
        dve.wait_ge(self.rstd, 1)
        for t in range(TT):
            dve.tensor_scalar(self.xn[:, t, :], self.x[:, t, :], self.mv[:, t, 0:1], self.rs[:, t:t + 1],
                              ALU.subtract, ALU.mult).then_inc(self.normed, 1)
        for t in range(TT):
            bank = self.banks[t % 2]
            cols = slice(t * P, (t + 1) * P)
            if len(self.out) == 1:
                dve.wait_ge(self.turned, t + 1)
                dve.tensor_copy(self.out[0][:, :, cols], bank[:, :].rearrange("p (k c) -> p k c", k=KC)).then_inc(self.done, 1)
            else:
                th, tl = self.out
                dve.wait_ge(self.high, t + 1)
                dve.scalar_tensor_tensor(out=tl[:, :, cols], in0=bank[:, :].rearrange("p (k c) -> p k c", k=KC), scalar=S_H,
                                         in1=th[:, :, cols], op0=ALU.mult, op1=ALU.subtract).then_inc(self.done, 1)

    def scalar(self, act):
        act.wait_ge(self.moments, 2 * TT)
        act.activation(self.sd[:, :], self.mv[:, :, 1], ACT.Sqrt, bias=self.eps).then_inc(self.std, 1)
        if len(self.out) == 2:
            for t in range(TT):
                act.wait_ge(self.turned, t + 1)
                act.activation(self.out[0][:, :, t * P:(t + 1) * P], self.banks[t % 2][:, :].rearrange("p (k c) -> p k c", k=KC),
                               ACT.Copy, scale=S_H).then_inc(self.high, 1)

    def tensor(self, pe):
        for t in range(TT):
            pe.wait_ge(self.normed, t + 1)
            wait(pe, self.done, t - 1)
            for k in range(KC):
                mm = pe.transpose(self.banks[t % 2][:, k * P:(k + 1) * P], self.xn[:, t, k * P:(k + 1) * P], self.ident)
            mm.then_inc(self.turned, 1)


def identity(pool, ident, sem):
    pool.memset(ident, 0.0).then_inc(sem, 1)
    pool.wait_ge(sem, 1)
    pool.affine_select(out=ident, in_=ident, compare_op=ALU.not_equal, fill=1.0, base=0,
                       pattern=[[-1, P]], channel_multiplier=1).then_inc(sem, 1)


def queries(nc, x, wqT, norm_w, q_hi, q_lo, kvT, ctxT, kv_parts, ctx_parts, stored):
    with ExitStack() as ctx:
        def sb(name, shape, dt):
            return ctx.enter_context(nc.sbuf_tensor(name, shape, dt))

        def sem(name):
            return ctx.enter_context(nc.semaphore(name))

        GR = HEADS // 4
        xs = sb("q_x", [P, TT, HID], F32)
        ident = sb("q_ident", [P, P], F32)
        eps = sb("q_eps", [P, 1], F32)
        eps2 = sb("q_eps2", [P, 1], F32)
        nw = sb("q_nw", [P, 2], F32)
        nwp = sb("q_nwp", [P, 1], F32)
        th = sb("q_th", [P, KC, ND], F16)
        tl = sb("q_tl", [P, KC, ND], F16)
        wst = sb("q_wst", [P, 2, KC, 512], F32)
        wh = sb("q_wh", [P, 2, KC, 512], F16)
        wl = sb("q_wl", [P, 2, KC, 512], F16)
        sq = sb("q_sq", [P, 2, 512], F32)
        ss = sb("q_ss", [P, 2, 4], F32)
        sd = sb("q_sd", [P, 2, 4], F32)
        rs = sb("q_rs", [P, 2, 4], F32)
        qs = sb("q_qs", [P, TT, 512], F32)
        kvst = sb("q_kvst", [P, 2, KC, 512], F32)
        kv_h, kv_l = kv_parts
        ctx_f, ctx_h, ctx_l = ctx_parts
        qh = sb("q_qh", [P, 2, BATCH, 4 * TOK], F16)
        ql = sb("q_ql", [P, 2, BATCH, 4 * TOK], F16)
        pT = [ctx.enter_context(nc.psum_tensor(f"q_pT{i}", [P, 512], F32)) for i in range(2)]
        pQ = [ctx.enter_context(nc.psum_tensor(f"q_pQ{i}", [P, 512], F32)) for i in range(TT)]
        pR = [ctx.enter_context(nc.psum_tensor(f"q_pR{i}", [P, 512], F32)) for i in range(2)]

        x_in = sem("q_x_in")
        nw_in = sem("q_nw_in")
        consts = sem("q_consts")
        idt = sem("q_idt")
        w_in = [sem(f"q_w_in{i}") for i in range(2)]
        w_hi = sem("q_w_hi")
        w_lo = sem("q_w_lo")
        q_ok = sem("q_q_ok")
        sq_ok = sem("q_sq_ok")
        ss_ok = sem("q_ss_ok")
        sd_ok = sem("q_sd_ok")
        rs_ok = sem("q_rs_ok")
        qs_ok = sem("q_qs_ok")
        t_ok = sem("q_t_ok")
        hi_ok = sem("q_hi_ok")
        lo_ok = sem("q_lo_ok")
        kv_in = [sem(f"q_kv_in{i}") for i in range(2)]
        kv_hi = sem("q_kv_hi")
        kv_lo = sem("q_kv_lo")
        ctx_in = [sem(f"q_ctx_in{n}") for n in range(NCH)]
        ctx_hi = sem("q_ctx_hi")
        ctx_lo = sem("q_ctx_lo")
        ln = LayerNorm(nc, ctx, "qln", xs, ident[:, :], eps[:, 0:1], pT, (th, tl))
        block = ctx.enter_context(nc.Block())

        def loop(eng, body):
            for j in range(2):
                body(0, j)
            with eng.Fori(1, GR // 2 - 1) as pair:
                for j in range(2):
                    body(pair, j)
            for j in range(2):
                body(GR // 2 - 1, j)

        LAG = 2

        def earlier(pair, j, t):
            if t >= LAG:
                return pair, j, t - LAG
            if j:
                return pair, 0, t - LAG + TT
            return None if isinstance(pair, int) and pair == 0 else (pair - 1, 1, t - LAG + TT)

        def gap_jobs(pair, j, t):
            if not isinstance(pair, int):
                return []
            if pair == 0:
                return [("W", j)] if t == 3 else []
            return [[("W", 2)], [], [("W", 3)], [], [("C", 0)], [("C", 1)], [("C", 2)], [("C", 3)]][4 * j + t]

        @block.sync
        def _(sp):
            sp.dma_start(xs[:, :, :], x.rearrange("(t p) c -> p t c", p=P)).then_inc(x_in, 16)
            sp.dma_start(nw[:, :], norm_w).then_inc(nw_in, 16)

            def body(pair, j):
                g = 2 * pair + j
                wait(sp, w_lo, g - 1)
                src = wqT[:, g * 512:(g + 1) * 512] if isinstance(g, int) else wqT[:, bass.ds(g * 512, 512)]
                sp.dma_start(wst[:, j, :, :], src.rearrange("(k p) c -> p k c", p=P)).then_inc(w_in[j], 16)

            def load_kv(n):
                sp.dma_start(kvst[:, n % 2, :, :], kvT[n // 2][:, 512 * (n % 2):512 * (n % 2) + 512]
                             .rearrange("(k p) c -> p k c", p=P)).then_inc(kv_in[n % 2], 16)

            for j in range(2):
                body(0, j)
            for n in range(2):
                load_kv(n)
            for n, (c0, w) in enumerate(CH):
                sp.dma_start(ctx_f[:, :, c0:c0 + w], ctxT[0][:, c0:c0 + w].rearrange("(k p) c -> p k c", p=P)).then_inc(ctx_in[n], 16)
            with sp.Fori(1, GR // 2 - 1) as pair:
                for j in range(2):
                    body(pair, j)
            for n in range(2):
                sp.wait_ge(kv_lo, n + 1)
                load_kv(2 + n)
            for j in range(2):
                body(GR // 2 - 1, j)

        @block.gpsimd
        def _(pool):
            identity(pool, ident[:, :], idt)

            def body(pair, j):
                g = 2 * pair + j
                wait(pool, lo_ok, TT * (g + 1))
                for dram, st in ((q_hi, qh), (q_lo, ql)):
                    dst = dram[:, :, g * 256:(g + 1) * 256] if isinstance(g, int) else dram[:, :, bass.ds(g * 256, 256)]
                    pool.dma_start(dst.rearrange("b p c -> p b c"), st[:, j, :, :]).then_inc(stored[j], 16)
            loop(pool, body)

        @block.tensor
        def _(pe):
            pe.wait_ge(idt, 2)
            ln.tensor(pe)
            pe.wait_ge(ln.done, TT)

            def turn(pair, j, t):
                n = TT * (2 * pair + j) + t
                wait(pe, qs_ok, n + 1)
                wait(pe, lo_ok, n - 1)
                for h in range(4):
                    mm = pe.transpose(pR[t % 2][:, h * P:(h + 1) * P], qs[:, t, h * P:(h + 1) * P], ident[:, :])
                mm.then_inc(t_ok, 1)

            def body(pair, j):
                g = 2 * pair + j
                wait(pe, w_lo, g + 1)
                for t in range(TT):
                    n = TT * g + t
                    wait(pe, qs_ok, n - TT + 1)
                    for k in range(KC):
                        mm = split3(pe, pQ[t][:, :], (th[:, k, t * P:(t + 1) * P], tl[:, k, t * P:(t + 1) * P]),
                                    (wh[:, j, k, :], wl[:, j, k, :]), k == 0, k == KC - 1)
                    mm.then_inc(q_ok, 1)
                    if earlier(pair, j, t):
                        turn(*earlier(pair, j, t))
            loop(pe, body)
            for t in range(TT - LAG, TT):
                turn(GR // 2 - 1, 1, t)

        @block.scalar
        def _(act):
            def high(pair, j, t):
                n = TT * (2 * pair + j) + t
                if t == 0:
                    wait(act, stored[j], 32 * pair)
                wait(act, t_ok, n + 1)
                if isinstance(pair, int) and pair == 0 and j == 0 and t == 0:
                    act.wait_ge(consts, 3)
                out = qh[:, j, 2 * t:2 * t + 2, :].rearrange("p b (h q) -> p h b q", h=4)
                act.activation(out, pR[t % 2][:, :].rearrange("p (h b q) -> p h b q", h=4, b=2), ACT.Copy,
                               scale=nwp[:, 0:1]).then_inc(hi_ok, 1)

            def split(pair, j):
                g = 2 * pair + j
                wait(act, w_in[j], 16 * (pair + 1))
                wait(act, q_ok, TT * (g - 1))
                act.activation(wh[:, j, :, :], wst[:, j, :, :], ACT.Copy, scale=S_W).then_inc(w_hi, 1)

            def gap_split(kind, n):
                if kind == "W":
                    act.wait_ge(kv_in[n % 2], 16 * (n // 2 + 1))
                    act.activation(kv_h[:, n // 2, :, 512 * (n % 2):512 * (n % 2) + 512], kvst[:, n % 2, :, :],
                                   ACT.Copy, scale=S_W).then_inc(kv_hi, 1)
                else:
                    c0, w = CH[n]
                    act.wait_ge(ctx_in[n], 16)
                    act.activation(ctx_h[:, :, c0:c0 + w], ctx_f[:, :, c0:c0 + w], ACT.Copy, scale=S_CTX).then_inc(ctx_hi, 1)

            act.wait_ge(consts, 2)
            ln.scalar(act)
            split(0, 0)

            def body(pair, j):
                g = 2 * pair + j
                for t in range(TT):
                    if t == 2 and not (isinstance(g, int) and g == GR - 1):
                        split(pair + j, 1 - j)
                    n = TT * g + t
                    wait(act, q_ok, n + 1)
                    wait(act, ss_ok, n - 1)
                    act.activation(sq[:, t % 2, :], pQ[t][:, :], ACT.Square, scale=1.0 / (S_H * S_W)).then_inc(sq_ok, 1)
                    wait(act, ss_ok, n + 1)
                    wait(act, rs_ok, n - 1)
                    act.activation(sd[:, t % 2, :], ss[:, t % 2, :], ACT.Sqrt, bias=eps2[:, 0:1],
                                   scale=(S_H * S_W / S_Q) ** 2 / HD).then_inc(sd_ok, 1)
                    if earlier(pair, j, t):
                        high(*earlier(pair, j, t))
                    for job in gap_jobs(pair, j, t):
                        gap_split(*job)
            loop(act, body)
            for t in range(TT - LAG, TT):
                high(GR // 2 - 1, 1, t)

        @block.vector
        def _(dve):
            dve.memset(eps[:, :], EPS).then_inc(consts, 1)
            dve.memset(eps2[:, :], EPS * (S_H * S_W / S_Q) ** 2).then_inc(consts, 1)
            dve.wait_ge(nw_in, 16)
            dve.tensor_tensor(nwp[:, :], nw[:, 0:1], nw[:, 1:2], ALU.mult).then_inc(consts, 1)
            dve.wait_ge(x_in, 16)
            ln.vector(dve)

            def split(pair, j):
                wait(dve, w_hi, 2 * pair + j + 1)
                dve.scalar_tensor_tensor(out=wl[:, j, :, :], in0=wst[:, j, :, :], scalar=S_W, in1=wh[:, j, :, :],
                                         op0=ALU.mult, op1=ALU.subtract).then_inc(w_lo, 1)

            def gap_split(kind, n):
                if kind == "W":
                    cols = slice(512 * (n % 2), 512 * (n % 2) + 512)
                    dve.wait_ge(kv_hi, n + 1)
                    dve.scalar_tensor_tensor(out=kv_l[:, n // 2, :, cols], in0=kvst[:, n % 2, :, :], scalar=S_W,
                                             in1=kv_h[:, n // 2, :, cols], op0=ALU.mult, op1=ALU.subtract).then_inc(kv_lo, 1)
                else:
                    c0, w = CH[n]
                    dve.wait_ge(ctx_hi, n + 1)
                    dve.scalar_tensor_tensor(out=ctx_l[:, :, c0:c0 + w], in0=ctx_f[:, :, c0:c0 + w], scalar=S_CTX,
                                             in1=ctx_h[:, :, c0:c0 + w], op0=ALU.mult, op1=ALU.subtract).then_inc(ctx_lo, 1)

            split(0, 0)

            def low(pair, j, t):
                n = TT * (2 * pair + j) + t
                wait(dve, hi_ok, n + 1)
                dve.wait_ge(consts, 3)
                out = ql[:, j, 2 * t:2 * t + 2, :].rearrange("p b (h q) -> p b h q", h=4)
                hi = qh[:, j, 2 * t:2 * t + 2, :].rearrange("p b (h q) -> p b h q", h=4)
                src = pR[t % 2][:, :].rearrange("p (h b q) -> p b h q", h=4, b=2)
                for b in range(2):
                    mm = dve.scalar_tensor_tensor(out=out[:, b, :, :], in0=src[:, b, :, :], scalar=nwp[:, 0:1],
                                                  in1=hi[:, b, :, :], op0=ALU.mult, op1=ALU.subtract)
                mm.then_inc(lo_ok, 1)

            def body(pair, j):
                g = 2 * pair + j
                for t in range(TT):
                    n = TT * g + t
                    if t == 2 and not (isinstance(g, int) and g == GR - 1):
                        split(pair + j, 1 - j)
                    wait(dve, sq_ok, n + 1)
                    dve.tensor_reduce(ss[:, t % 2, :], sq[:, t % 2, :].rearrange("p (h c) -> p h c", h=4), AX.X, ALU.add).then_inc(ss_ok, 1)
                    wait(dve, sd_ok, n + 1)
                    dve.reciprocal(rs[:, t % 2, :], sd[:, t % 2, :]).then_inc(rs_ok, 1)
                    wait(dve, rs_ok, n + 1)
                    wait(dve, t_ok, n - TT + 1)
                    dve.tensor_tensor(qs[:, t, :].rearrange("p (h c) -> p h c", h=4),
                                      pQ[t][:, :].rearrange("p (h c) -> p h c", h=4),
                                      rs[:, t % 2, :].unsqueeze(2).to_broadcast([P, 4, HD]), ALU.mult).then_inc(qs_ok, 1)
                    if earlier(pair, j, t):
                        low(*earlier(pair, j, t))
                    for job in gap_jobs(pair, j, t):
                        gap_split(*job)
            loop(dve, body)
            for t in range(TT - LAG, TT):
                low(GR // 2 - 1, 1, t)


def output_projection(nc, x, woT, o_dram, x1):
    with ExitStack() as ctx:
        def sb(name, shape, dt):
            return ctx.enter_context(nc.sbuf_tensor(name, shape, dt))

        def sem(name):
            return ctx.enter_context(nc.semaphore(name))

        GR = HEADS // 4
        xs = sb("p_x", [P, TT, HID], F32)
        ost = sb("p_ost", [P, 2, BATCH, 4 * TOK], F32)
        wst = sb("p_wst", [P, 2, 4, HID], F32)
        oh = sb("p_oh", [P, 2, 4, ND], F16)
        ol = sb("p_ol", [P, 2, 4, ND], F16)
        wh = sb("p_wh", [P, 2, 4, HID], F16)
        wl = sb("p_wl", [P, 2, 4, HID], F16)
        pO = [ctx.enter_context(nc.psum_tensor(f"p_pO{i}", [P, HID], F32)) for i in range(TT)]
        x_in = sem("p_x_in")
        g_in = [sem(f"p_g_in{i}") for i in range(2)]
        hi = sem("p_hi")
        lo = sem("p_lo")
        made = sem("p_made")
        added = sem("p_added")
        block = ctx.enter_context(nc.Block())

        def loop(eng, body):
            for j in range(2):
                body(0, j)
            with eng.Fori(1, GR // 2 - 1) as pair:
                for j in range(2):
                    body(pair, j)
            for j in range(2):
                body(GR // 2 - 1, j)

        @block.sync
        def _(sp):
            def body(pair, j):
                g = 2 * pair + j
                wait(sp, lo, 2 * (g - 1))
                if isinstance(g, int):
                    so, sw = o_dram[:, :, g * 256:(g + 1) * 256], woT[g * 512:(g + 1) * 512, :]
                else:
                    so, sw = o_dram[:, :, bass.ds(g * 256, 256)], woT[bass.ds(g * 512, 512), :]
                sp.dma_start(ost[:, j, :, :], so.rearrange("b p c -> p b c")).then_inc(g_in[j], 16)
                sp.dma_start(wst[:, j, :, :], sw.rearrange("(h p) c -> p h c", p=P)).then_inc(g_in[j], 16)
            loop(sp, body)
            sp.dma_start(xs[:, :, :], x.rearrange("(t p) c -> p t c", p=P)).then_inc(x_in, 16)

        @block.scalar
        def _(act):
            def body(pair, j):
                g = 2 * pair + j
                wait(act, g_in[j], 32 * (pair + 1))
                wait(act, made, g - 1)
                act.activation(oh[:, j, :, :].rearrange("p h (b q) -> p h b q", b=BATCH),
                               ost[:, j, :, :].rearrange("p b (h q) -> p h b q", h=4), ACT.Copy, scale=S_O).then_inc(hi, 1)
                act.activation(wh[:, j, :, :], wst[:, j, :, :], ACT.Copy, scale=S_W).then_inc(hi, 1)
            loop(act, body)

        @block.vector
        def _(dve):
            def body(pair, j):
                g = 2 * pair + j
                wait(dve, hi, 2 * g + 1)
                for h in range(4):
                    v = ost[:, j, :, :].rearrange("p b (h q) -> p h b q", h=4)[:, h, :, :]
                    i = dve.scalar_tensor_tensor(out=ol[:, j, h, :].rearrange("p (b q) -> p b q", b=BATCH), in0=v, scalar=S_O,
                                                 in1=oh[:, j, h, :].rearrange("p (b q) -> p b q", b=BATCH),
                                                 op0=ALU.mult, op1=ALU.subtract)
                i.then_inc(lo, 1)
                wait(dve, hi, 2 * g + 2)
                dve.scalar_tensor_tensor(out=wl[:, j, :, :], in0=wst[:, j, :, :], scalar=S_W, in1=wh[:, j, :, :],
                                         op0=ALU.mult, op1=ALU.subtract).then_inc(lo, 1)
            loop(dve, body)
            dve.wait_ge(x_in, 16)
            dve.wait_ge(made, GR)
            for t in range(TT):
                dve.scalar_tensor_tensor(out=x1[:, t, :], in0=pO[t][:, :], scalar=1.0 / (S_O * S_W), in1=xs[:, t, :],
                                         op0=ALU.mult, op1=ALU.add).then_inc(added, 1)

        @block.tensor
        def _(pe):
            def body(pair, j):
                g = 2 * pair + j
                wait(pe, lo, 2 * (g + 1))
                first = isinstance(g, int) and g == 0
                final = isinstance(g, int) and g == GR - 1
                for t in range(TT):
                    for h in range(4):
                        mm = split3(pe, pO[t][:, :], (oh[:, j, h, t * P:(t + 1) * P], ol[:, j, h, t * P:(t + 1) * P]),
                                    (wh[:, j, h, :], wl[:, j, h, :]), first and h == 0, final and h == 3)
                mm.then_inc(made, 1)
            loop(pe, body)


def state_space(nc, winG, wdtT, woutG, params, heads_par, x1):
    with ExitStack() as ctx:
        def sb(name, shape, dt=F32):
            return ctx.enter_context(nc.sbuf_tensor(name, shape, dt))

        def sem(name):
            return ctx.enter_context(nc.semaphore("m_" + name))

        G = GROUPS
        NIN = CONV + GCH
        CW = CONV * P
        ident = sb("m_ident", [P, P])
        ones = sb("m_ones", [P, P])
        upto = sb("m_upto", [P, P])
        after = sb("m_after", [P, P])
        eps = sb("m_eps", [P, 1])
        th = sb("m_th", [P, KC, ND], F16)
        tl = sb("m_tl", [P, KC, ND], F16)
        wst = sb("m_wst", [P, KC, NIN * P])
        wh = sb("m_wh", [P, KC, NIN * P], F16)
        wl = sb("m_wl", [P, KC, NIN * P], F16)
        wost = sb("m_wost", [P, GCH, HID])
        woh = sb("m_woh", [P, GCH, HID], F16)
        wol = sb("m_wol", [P, GCH, HID], F16)
        wdt = sb("m_wdt", [P, KC, SSM_HEADS])
        wdh = sb("m_wdh", [P, KC, SSM_HEADS], F16)
        wdl = sb("m_wdl", [P, KC, SSM_HEADS], F16)
        hp = sb("m_hp", [P, 2, SSM_HEADS])
        par = sb("m_par", [P, 2, NPAR])
        sp_ = [sb(f"m_sp{i}", [P, TT, SSM_HEADS]) for i in range(6)]
        dt = sb("m_dt", [P, TT, SSM_HEADS])
        a = sb("m_a", [P, TT, SSM_HEADS])
        dtg = sb("m_dtg", [P, TT, GH])
        ag = sb("m_ag", [P, TT, GH])
        cv = sb("m_cv", [P, 2, ND])
        xc = sb("m_xc", [P, CONV, ND])
        gate = sb("m_gate", [P, GCH, ND])
        dtx = sb("m_dtx", [P, 2, GH * SSM_P])
        cbm = sb("m_cbm", [P, 2, P])
        R = sb("m_R", [P, 2, 4, P])
        E = sb("m_E", [P, 4, 4, P])
        y = sb("m_y", [P, GCH, ND])
        sqb = sb("m_sqb", [P, 2, ND])
        sd = sb("m_sd", [P, ND])
        rs = sb("m_rs", [P, ND])
        yh = sb("m_yh", [P, GCH, ND], F16)
        yl = sb("m_yl", [P, GCH, ND], F16)
        bank = [ctx.enter_context(nc.psum_tensor(f"m_b{i}", [P, 512], F32)) for i in range(8)]
        pI, pX, pCB, pD, pY, pO, pS = bank[0:2], bank[2], bank[3], bank[4], bank[5], bank[6], bank[7]

        (idt, cst, wdt_in, hp_in, wdt_hi, wdt_lo, dtp, sp_dve, sp_act, dt_ok, wA_in, wB_in, wC_in, wA_hi, wA_lo, wB_hi, wB_lo,
         wC_hi, wC_lo, ip, cv0, cvs, conv, silu, gat, agc, xt, dx, cb, cm, r_ok, d_ok, e_ok, m_ok, y_ok, yev, sqy, ssm,
         sdy, rsy, gr, yg, yhi, ylo, op, acc) = [sem(n) for n in (
             "idt cst wdt_in hp_in wdt_hi wdt_lo dtp sp_dve sp_act dt_ok wA_in wB_in wC_in wA_hi wA_lo wB_hi wB_lo "
             "wC_hi wC_lo ip cv0 cvs conv silu gat agc xt dx cb cm r_ok d_ok e_ok m_ok y_ok yev sqy ssm "
             "sdy rsy gr yg yhi ylo op acc").split()]
        par_in = sem("par_in")
        taps = sem("taps")
        ln = LayerNorm(nc, ctx, "mln", x1, ident[:, :], eps[:, 0:1], pI, (th, tl))
        block = ctx.enter_context(nc.Block())

        def loop(eng, body):
            body(0)
            with eng.Fori(1, G - 1) as g:
                body(g)
            body(G - 1)

        def at_last(g):
            return isinstance(g, int) and g == G - 1

        def at_first(g):
            return isinstance(g, int) and g == 0

        @block.sync
        def _(sp):
            sp.dma_start(wdt[:, :, :], wdtT.rearrange("(k p) c -> p k c", p=P)).then_inc(wdt_in, 16)
            sp.dma_start(hp[:, :, :], heads_par).then_inc(hp_in, 16)

            def body(g):
                w = row(winG, g)
                wait(sp, wA_lo, g)
                sp.dma_start(wst[:, :, 0:CW], w[:, 0:CW].rearrange("(k p) c -> p k c", p=P)).then_inc(wA_in, 16)
                wait(sp, wB_lo, g)
                sp.dma_start(wst[:, :, CW:NIN * P], w[:, CW:NIN * P].rearrange("(k p) c -> p k c", p=P)).then_inc(wB_in, 16)
                wait(sp, wC_lo, g)
                sp.dma_start(wost[:, :, :], row(woutG, g).rearrange("(k p) c -> p k c", p=P)).then_inc(wC_in, 16)
                wait(sp, yg, GCH * g)
                sp.dma_start(par[:, 0, :], row(params, g)).then_inc(par_in, 16)
            loop(sp, body)

        @block.gpsimd
        def _(pool):
            identity(pool, ident[:, :], idt)
            pool.memset(upto[:, :], 1.0).then_inc(idt, 1)
            pool.memset(after[:, :], 1.0).then_inc(idt, 1)
            pool.wait_ge(idt, 4)
            pool.affine_select(out=upto[:, :], in_=upto[:, :], compare_op=ALU.is_ge, fill=0.0, base=0,
                               pattern=[[1, P]], channel_multiplier=-1).then_inc(idt, 1)
            pool.affine_select(out=after[:, :], in_=after[:, :], compare_op=ALU.is_ge, fill=0.0, base=-1,
                               pattern=[[-1, P]], channel_multiplier=1).then_inc(idt, 1)
            pool.wait_ge(idt, 6)
            pool.affine_select(out=upto[:, TOK:P], in_=upto[:, TOK:P], compare_op=ALU.is_ge, fill=0.0, base=-TOK,
                               pattern=[[0, TOK]], channel_multiplier=1).then_inc(idt, 1)
            pool.affine_select(out=after[:, 0:TOK], in_=after[:, 0:TOK], compare_op=ALU.is_ge, fill=0.0, base=TOK - 1,
                               pattern=[[0, TOK]], channel_multiplier=-1).then_inc(idt, 1)
            pool.wait_ge(idt, 8)

            def body(g):
                for t in range(TT):
                    for q in range(2):
                        n = 8 * g + 2 * t + q
                        wait(pool, agc, 2 * (g + 1))
                        wait(pool, d_ok, n - 1)
                        pool.tensor_tensor(R[:, q, :, :], upto[:, :].unsqueeze(1).to_broadcast([P, 4, P]),
                                           ag[:, t, 4 * q:4 * q + 4].unsqueeze(2).to_broadcast([P, 4, P]), ALU.mult).then_inc(r_ok, 1)
                for j in range(GCH):
                    wait(pool, rsy, g + 1)
                    pool.tensor_tensor(gate[:, j, :], gate[:, j, :], rs[:, :], ALU.mult).then_inc(gr, 1)
            loop(pool, body)

        @block.tensor
        def _(pe):
            pe.wait_ge(idt, 8)
            ln.tensor(pe)
            pe.wait_ge(ln.done, TT)
            pe.wait_ge(wdt_lo, 1)
            for t in range(TT):
                for k in range(KC):
                    mm = split3(pe, pD[:, t * SSM_HEADS:(t + 1) * SSM_HEADS], (th[:, k, t * P:(t + 1) * P], tl[:, k, t * P:(t + 1) * P]),
                                (wdh[:, k, :], wdl[:, k, :]), k == 0, k == KC - 1)
            mm.then_inc(dtp, 1)

            def input_chunk(g, j):
                wait(pe, wA_lo if j < CONV else wB_lo, g + 1)
                if j < 2:
                    wait(pe, gat, GCH * (g - 1) + GCH - 1 + j)
                elif j < CONV + 2:
                    wait(pe, conv, CONV * g + j - 1)
                else:
                    wait(pe, gat, GCH * g + j - CONV - 1)
                for k in range(KC):
                    mm = split3(pe, pI[j % 2][:, :], (wh[:, k, j * P:(j + 1) * P], wl[:, k, j * P:(j + 1) * P]),
                                (th[:, k, :], tl[:, k, :]), k == 0, k == KC - 1)
                mm.then_inc(ip, 1)

            def out_tile(g, t):
                wait(pe, ylo, GCH * (g + 1))
                wait(pe, wC_lo, g + 1)
                wait(pe, acc, TT * (g + 1) + t)
                for j in range(GCH):
                    mm = split3(pe, pO[:, :], (yh[:, j, t * P:(t + 1) * P], yl[:, j, t * P:(t + 1) * P]),
                                (woh[:, j, :], wol[:, j, :]), j == 0, j == GCH - 1)
                mm.then_inc(op, 1)

            def decay(g, t, q):
                n = 8 * g + 2 * t + q
                wait(pe, r_ok, n + 1)
                wait(pe, e_ok, n)
                if at_first(g) and n == 0:
                    pe.wait_ge(dt_ok, 1)
                pe.matmul(pD[:, :], after[:, :], R[:, q, :, :], start=True, stop=True).then_inc(d_ok, 1)

            def outputs(g, t):
                wait(pe, m_ok, 8 * g + 2 * t + 2)
                wait(pe, dx, TT * g + t + 1)
                wait(pe, yev, TT * g + t)
                for h in range(GH):
                    mm = pe.matmul(pY[64 * (h % 2):64 * (h % 2) + 64, (h // 2) * P:(h // 2) * P + P],
                                   dtx[:, t % 2, h * SSM_P:(h + 1) * SSM_P], E[:, 2 * (t % 2) + h // 4, h % 4, :],
                                   start=True, stop=True)
                mm.then_inc(y_ok, 1)

            def body(g):
                for j in range(NIN):
                    input_chunk(g, j)
                for t in range(TT):
                    cols = slice(t * P, (t + 1) * P)
                    wait(pe, silu, CONV * (g + 1))
                    wait(pe, dx, TT * g + t)
                    for j in range(GCH):
                        mm = pe.transpose(pX[:, j * P:(j + 1) * P], xc[:, j, cols], ident[:, :])
                    mm.then_inc(xt, 1)
                    wait(pe, cm, TT * g + t)
                    pe.matmul(pCB[:, 0:P], xc[:, GCH, cols], xc[:, GCH + 1, cols], start=True, stop=True).then_inc(cb, 1)
                    decay(g, t, 0)
                    if not at_first(g):
                        out_tile(g - 1, t)
                    decay(g, t, 1)
                    if t:
                        outputs(g, t - 1)
                outputs(g, TT - 1)
                for j in range(GCH):
                    wait(pe, sqy, GCH * g + j + 1)
                    if j == 0:
                        wait(pe, sdy, g)
                    pe.matmul(pS[:, :], ones[:, :], sqb[:, j % 2, :], start=j == 0, stop=j == GCH - 1).then_inc(ssm, 1)
            loop(pe, body)
            for t in range(TT):
                out_tile(G - 1, t)

        @block.scalar
        def _(act):
            act.wait_ge(wdt_in, 16)
            act.activation(wdh[:, :, :], wdt[:, :, :], ACT.Copy, scale=S_W).then_inc(wdt_hi, 1)
            act.wait_ge(cst, 1)
            ln.scalar(act)

            def split(g, part):
                if part == "A":
                    wait(act, wA_in, 16 * (g + 1))
                    wait(act, ip, NIN * (g - 1) + CONV)
                    c = slice(0, CW)
                    act.activation(wh[:, :, c], wst[:, :, c], ACT.Copy, scale=S_W).then_inc(wA_hi, 1)
                elif part == "B":
                    wait(act, wB_in, 16 * (g + 1))
                    wait(act, ip, NIN * g)
                    c = slice(CW, NIN * P)
                    act.activation(wh[:, :, c], wst[:, :, c], ACT.Copy, scale=S_W).then_inc(wB_hi, 1)
                else:
                    wait(act, wC_in, 16 * (g + 1))
                    wait(act, op, TT * g)
                    act.activation(woh[:, :, :], wost[:, :, :], ACT.Copy, scale=S_W).then_inc(wC_hi, 1)

            split(0, "A")
            split(0, "B")
            act.wait_ge(sp_dve, 2)
            act.activation(sp_[2][:, :, :], sp_[1][:, :, :], ACT.Exp).then_inc(sp_act, 1)
            act.wait_ge(hp_in, 16)
            act.activation(hp[:, 1, :], hp[:, 1, :], ACT.Exp).then_inc(sp_act, 1)
            act.wait_ge(sp_dve, 3)
            act.activation(sp_[4][:, :, :], sp_[3][:, :, :], ACT.Ln).then_inc(sp_act, 1)

            def finish_conv(g, j):
                wait(act, conv, CONV * g + j + 1)
                if j == 0:
                    wait(act, yev, TT * g)
                act.activation(xc[:, j, :], cv[:, j % 2, :], ACT.Silu).then_inc(silu, 1)

            def body(g):
                wait(act, taps, g + 1)
                for j in range(CONV):
                    wait(act, ip, NIN * g + j + 1)
                    wait(act, silu, CONV * g + j - 1)
                    act.activation(cv[:, j % 2, :], pI[j % 2][:, :], ACT.Identity,
                                   bias=par[:, 0, CONV * TAPS + j:CONV * TAPS + j + 1],
                                   scale=par[:, 1, j * TAPS + TAPS - 1:j * TAPS + TAPS]).then_inc(cv0, 1)
                    if j:
                        finish_conv(g, j - 1)
                finish_conv(g, CONV - 1)
                for j in range(GCH):
                    wait(act, ip, NIN * g + CONV + j + 1)
                    if j == 0:
                        wait(act, yg, GCH * g)
                    act.activation(gate[:, j, :], pI[j % 2][:, :], ACT.Silu, scale=1.0 / (S_H * S_W)).then_inc(gat, 1)
                for t in range(TT):
                    for q in range(2):
                        n = 8 * g + 2 * t + q
                        wait(act, d_ok, n + 1)
                        wait(act, y_ok, TT * g + t - 1)
                        act.activation(E[:, 2 * (t % 2) + q, :, :], pD[:, :].rearrange("p (h c) -> p h c", h=4), ACT.Exp).then_inc(e_ok, 1)
                if not at_last(g):
                    split(g + 1, "A")
                    split(g + 1, "B")
                split(g, "C")
                wait(act, yev, TT * (g + 1))
                for j in range(GCH):
                    wait(act, ssm, GCH * g + j - 1)
                    act.activation(sqb[:, j % 2, :], y[:, j, :], ACT.Square).then_inc(sqy, 1)
                wait(act, ssm, GCH * (g + 1))
                wait(act, rsy, g)
                act.activation(sd[:, :], pS[:, :], ACT.Sqrt, bias=eps[:, 0:1], scale=1.0 / (GCH * P)).then_inc(sdy, 1)
                for j in range(GCH):
                    wait(act, yg, GCH * g + j + 1)
                    wait(act, op, TT * g)
                    act.activation(yh[:, j, :], y[:, j, :], ACT.Copy, scale=S_Y).then_inc(yhi, 1)
            loop(act, body)

        @block.vector
        def _(dve):
            dve.memset(eps[:, :], EPS)
            dve.memset(ones[:, :], 1.0).then_inc(cst, 1)
            ln.vector(dve)
            dve.sem_inc(acc, TT)
            dve.wait_ge(wdt_hi, 1)
            dve.scalar_tensor_tensor(out=wdl[:, :, :], in0=wdt[:, :, :], scalar=S_W, in1=wdh[:, :, :],
                                     op0=ALU.mult, op1=ALU.subtract).then_inc(wdt_lo, 1)

            def split(g, part):
                if part == "A":
                    wait(dve, wA_hi, g + 1)
                    c = slice(0, CW)
                    dve.scalar_tensor_tensor(out=wl[:, :, c], in0=wst[:, :, c], scalar=S_W, in1=wh[:, :, c],
                                             op0=ALU.mult, op1=ALU.subtract).then_inc(wA_lo, 1)
                elif part == "B":
                    wait(dve, wB_hi, g + 1)
                    c = slice(CW, NIN * P)
                    dve.scalar_tensor_tensor(out=wl[:, :, c], in0=wst[:, :, c], scalar=S_W, in1=wh[:, :, c],
                                             op0=ALU.mult, op1=ALU.subtract).then_inc(wB_lo, 1)
                else:
                    wait(dve, wC_hi, g + 1)
                    dve.scalar_tensor_tensor(out=wol[:, :, :], in0=wost[:, :, :], scalar=S_W, in1=woh[:, :, :],
                                             op0=ALU.mult, op1=ALU.subtract).then_inc(wC_lo, 1)

            split(0, "A")
            split(0, "B")
            v, nv, e, u1, lnu, tmp = [x_[:, :, :] for x_ in sp_]
            step = [0]

            def link(ins):
                step[0] += 1
                ins.then_inc(sp_dve, 1)
                dve.wait_ge(sp_dve, step[0])

            dve.wait_ge(dtp, 1)
            dve.wait_ge(hp_in, 16)
            link(dve.scalar_tensor_tensor(out=v, in0=pD[:, 0:TT * SSM_HEADS].rearrange("p (t h) -> p t h", t=TT), scalar=1.0 / (S_H * S_W),
                                          in1=hp[:, 0, :].unsqueeze(1).to_broadcast([P, TT, SSM_HEADS]), op0=ALU.mult, op1=ALU.add))
            link(dve.scalar_tensor_tensor(out=nv, in0=v, scalar=-1.0, in1=v, op0=ALU.mult, op1=ALU.min))
            dve.wait_ge(sp_act, 2)
            link(dve.tensor_scalar(u1, e, 1.0, None, ALU.add))
            dve.wait_ge(sp_act, 3)
            link(dve.tensor_scalar(u1, u1, 1.0, None, ALU.subtract))
            link(dve.tensor_scalar(tmp, u1, 0.0, None, ALU.is_equal))
            link(dve.tensor_tensor(lnu, lnu, tmp, ALU.add))
            link(dve.tensor_tensor(u1, u1, tmp, ALU.add))
            link(dve.reciprocal(tmp, u1))
            link(dve.tensor_tensor(tmp, tmp, lnu, ALU.mult))
            link(dve.tensor_tensor(tmp, tmp, e, ALU.mult))
            link(dve.scalar_tensor_tensor(out=dt[:, :, :], in0=v, scalar=0.0, in1=tmp, op0=ALU.max, op1=ALU.add))
            link(dve.tensor_tensor(a[:, :, :], dt[:, :, :], hp[:, 1, :].unsqueeze(1).to_broadcast([P, TT, SSM_HEADS]), ALU.mult))
            link(dve.tensor_scalar(a[:, :, :], a[:, :, :], -1.0, -1.0e4, ALU.mult, ALU.max))
            dve.nop().then_inc(dt_ok, 1)

            def y_out(g, t):
                wait(dve, y_ok, TT * g + t + 1)
                wait(dve, yhi, GCH * g)
                wait(dve, ylo, GCH * g)
                cols = slice(t * P, (t + 1) * P)
                for j in range(GCH):
                    d = par[:, 0, CONV * TAPS + CONV + j:CONV * TAPS + CONV + j + 1]
                    i = dve.scalar_tensor_tensor(out=y[:, j, cols], in0=xc[:, j, cols], scalar=d, in1=pY[:, j * P:(j + 1) * P],
                                                 op0=ALU.mult, op1=ALU.add)
                i.then_inc(yev, 1)

            def accumulate(g, t):
                wait(dve, op, TT * g + t + 1)
                wait(dve, acc, TT * g + t + 1)
                dve.scalar_tensor_tensor(out=x1[:, t, :], in0=pO[:, :], scalar=1.0 / (S_Y * S_W), in1=x1[:, t, :],
                                         op0=ALU.mult, op1=ALU.add).then_inc(acc, 1)

            def body(g):
                wait(dve, par_in, 16 * (g + 1))
                dve.tensor_scalar(par[:, 1, 0:CONV * TAPS], par[:, 0, 0:CONV * TAPS], 1.0 / (S_H * S_W), None, ALU.mult).then_inc(taps, 1)
                wait(dve, taps, g + 1)
                for j in range(CONV):
                    n = CONV * g + j
                    wait(dve, cv0, n + 1)
                    acc_v = cv[:, j % 2, :].rearrange("p (b q) -> p b q", b=BATCH)
                    src = pI[j % 2][:, :].rearrange("p (b q) -> p b q", b=BATCH)
                    for m in range(1, TAPS):
                        if m > 1:
                            wait(dve, cvs, 2 * n + m - 1)
                        tap = par[:, 1, j * TAPS + TAPS - 1 - m:j * TAPS + TAPS - m]
                        i = dve.scalar_tensor_tensor(out=acc_v[:, :, m:], in0=src[:, :, 0:TOK - m], scalar=tap, in1=acc_v[:, :, m:],
                                                     op0=ALU.mult, op1=ALU.add)
                        i.then_inc(cvs if m < TAPS - 1 else conv, 1)
                hd = slice(GH * g, GH * g + GH) if isinstance(g, int) else bass.ds(g * GH, GH)
                wait(dve, r_ok, 8 * g)
                dve.tensor_copy(ag[:, :, :], a[:, :, hd]).then_inc(agc, 1)
                wait(dve, dx, TT * g)
                dve.tensor_copy(dtg[:, :, :], dt[:, :, hd]).then_inc(agc, 1)
                wait(dve, agc, 2 * (g + 1))
                for t in range(TT):
                    wait(dve, xt, TT * g + t + 1)
                    wait(dve, y_ok, TT * g + t - 1)
                    dve.tensor_tensor(dtx[:, t % 2, :].rearrange("p (h c) -> p h c", h=GH), pX[:, :].rearrange("p (h c) -> p h c", h=GH),
                                      dtg[:, t, :].unsqueeze(2).to_broadcast([P, GH, SSM_P]), ALU.mult).then_inc(dx, 1)
                    wait(dve, cb, TT * g + t + 1)
                    wait(dve, m_ok, 8 * g + 2 * t - 2)
                    dve.tensor_tensor(cbm[:, t % 2, :], pCB[:, 0:P], upto[:, :], ALU.mult).then_inc(cm, 1)
                    if not at_first(g):
                        accumulate(g - 1, t)
                    for q in range(2):
                        n = 8 * g + 2 * t + q
                        wait(dve, e_ok, n + 1)
                        wait(dve, cm, TT * g + t + 1)
                        Eb = E[:, 2 * (t % 2) + q, :, :]
                        dve.tensor_tensor(Eb, Eb, cbm[:, t % 2, :].unsqueeze(1).to_broadcast([P, 4, P]), ALU.mult).then_inc(m_ok, 1)
                    if t:
                        y_out(g, t - 1)
                y_out(g, TT - 1)
                if not at_last(g):
                    split(g + 1, "A")
                    split(g + 1, "B")
                split(g, "C")
                wait(dve, sdy, g + 1)
                wait(dve, gr, GCH * g)
                dve.reciprocal(rs[:, :], sd[:, :]).then_inc(rsy, 1)
                for j in range(GCH):
                    wait(dve, gr, GCH * g + j + 1)
                    nw = par[:, 0, CONV * TAPS + CONV + GCH + j:CONV * TAPS + CONV + GCH + j + 1]
                    dve.scalar_tensor_tensor(out=y[:, j, :], in0=y[:, j, :], scalar=nw, in1=gate[:, j, :],
                                             op0=ALU.mult, op1=ALU.mult).then_inc(yg, 1)
                for j in range(GCH):
                    wait(dve, yhi, GCH * g + j + 1)
                    dve.scalar_tensor_tensor(out=yl[:, j, :], in0=y[:, j, :], scalar=S_Y, in1=yh[:, j, :],
                                             op0=ALU.mult, op1=ALU.subtract).then_inc(ylo, 1)
            loop(dve, body)
            for t in range(TT):
                accumulate(G - 1, t)


def experts(nc, raT, bwT, out, x2):
    with ExitStack() as ctx:
        def sb(name, shape, dt=F32):
            return ctx.enter_context(nc.sbuf_tensor("f_" + name, shape, dt))

        def sem(name):
            return ctx.enter_context(nc.semaphore("f_" + name))

        N = EXPERTS + EXPERTS * RANK
        ident = sb("ident", [P, P])
        eps = sb("eps", [P, 1])
        hT = sb("hT", [P, KC, ND])
        ra = sb("ra", [P, KC, N])
        bw = sb("bw", [P, HID])
        lg = sb("lg", [P, TT, N])
        top = sb("top", [P, TT])
        eq = sb("eq", [P, TT, EXPERTS])
        pr = sb("pr", [P, TT, EXPERTS])
        rank = sb("rank", [P, EXPERTS])
        best = sb("best", [P, TT])
        wt = sb("wt", [P, TT, EXPERTS])
        wh = sb("wh", [P, TT, P])
        whT = sb("whT", [P, TT, P])
        bank = [ctx.enter_context(nc.psum_tensor(f"f_b{i}", [P, 512], F32)) for i in range(8)]
        w_in, idt, cst, lgp, chain, whp, wht, outp, added, stored = [
            sem(n) for n in "w_in idt cst lgp chain whp wht outp added stored".split()]
        ln = LayerNorm(nc, ctx, "fln", x2, ident[:, :], eps[:, 0:1], bank[0:2], (hT,))
        block = ctx.enter_context(nc.Block())

        @block.sync
        def _(sp):
            sp.dma_start(ra[:, :, :], raT.rearrange("(k p) c -> p k c", p=P)).then_inc(w_in, 16)
            sp.dma_start(bw[:, :], bwT).then_inc(w_in, 16)
            sp.wait_ge(added, TT)
            sp.dma_start(out.rearrange("(t p) c -> p t c", p=P), x2[:, :, :]).then_inc(stored, 16)
            sp.wait_ge(stored, 16)

        @block.gpsimd
        def _(pool):
            identity(pool, ident[:, :], idt)

        @block.scalar
        def _(act):
            act.wait_ge(cst, 1)
            ln.scalar(act)

        @block.tensor
        def _(pe):
            pe.wait_ge(idt, 2)
            ln.tensor(pe)
            pe.wait_ge(ln.done, TT)
            pe.wait_ge(w_in, 32)
            for t in range(TT):
                for k in range(KC):
                    mm = pe.matmul(bank[2 + t // 2][:, (t % 2) * 256:(t % 2) * 256 + N], hT[:, k, t * P:(t + 1) * P], ra[:, k, :],
                                   start=k == 0, stop=k == KC - 1)
            mm.then_inc(lgp, 1)
            pe.wait_ge(whp, 1)
            for t in range(TT):
                mm = pe.transpose(bank[0][:, t * P:(t + 1) * P], wh[:, t, :], ident[:, :])
            mm.then_inc(wht, 1)
            pe.wait_ge(whp, 2)
            for t in range(TT):
                pe.matmul(bank[4 + t][:, :], whT[:, t, :], bw[:, :], start=True, stop=True).then_inc(outp, 1)

        @block.vector
        def _(dve):
            dve.memset(eps[:, :], EPS).then_inc(cst, 1)
            for e in range(EXPERTS):
                i = dve.memset(rank[:, e:e + 1], float(EXPERTS - e))
            i.then_inc(cst, 1)
            ln.vector(dve)
            dve.wait_ge(cst, 2)
            step = [0]

            def link(ins):
                step[0] += 1
                ins.then_inc(chain, 1)
                dve.wait_ge(chain, step[0])

            dve.wait_ge(lgp, 1)
            for i in range(2):
                link(dve.tensor_copy(lg[:, 2 * i:2 * i + 2, :], bank[2 + i][:, :].rearrange("p (t c) -> p t c", t=2)[:, :, 0:N]))
            logits = lg[:, :, 0:EXPERTS]
            link(dve.tensor_reduce(top[:, :], logits, AX.X, ALU.max))
            topb = top[:, :].unsqueeze(2).to_broadcast([P, TT, EXPERTS])
            link(dve.tensor_tensor(eq[:, :, :], logits, topb, ALU.is_equal))
            link(dve.tensor_tensor(pr[:, :, :], eq[:, :, :], rank[:, :].unsqueeze(1).to_broadcast([P, TT, EXPERTS]), ALU.mult))
            link(dve.tensor_reduce(best[:, :], pr[:, :, :], AX.X, ALU.max))
            link(dve.tensor_tensor(eq[:, :, :], pr[:, :, :], best[:, :].unsqueeze(2).to_broadcast([P, TT, EXPERTS]), ALU.is_equal))
            link(dve.tensor_tensor(wt[:, :, :], eq[:, :, :], topb, ALU.mult))
            for t in range(TT):
                i = dve.tensor_tensor(wh[:, t, :].rearrange("p (e r) -> p e r", e=EXPERTS),
                                      lg[:, t, EXPERTS:N].rearrange("p (e r) -> p e r", e=EXPERTS),
                                      wt[:, t, :].unsqueeze(2).to_broadcast([P, EXPERTS, RANK]), ALU.mult)
            i.then_inc(whp, 1)
            dve.wait_ge(wht, 1)
            dve.tensor_copy(whT[:, :, :], bank[0][:, :].rearrange("p (t c) -> p t c", t=TT)).then_inc(whp, 1)
            for t in range(TT):
                dve.wait_ge(outp, t + 1)
                dve.tensor_tensor(x2[:, t, :], bank[4 + t][:, :], x2[:, t, :], ALU.add).then_inc(added, 1)


def perceiver_block(nc, x, ctxT, maskT, wqT, wkT, wvT, woT, norm_w, winG, wdtT, woutG, params, heads_par, raT, bwT, out):
    q_hi = nc.dram_tensor("q_hi_scratch", [BATCH, P, HEADS * TOK], F16, kind="Internal").ap()
    q_lo = nc.dram_tensor("q_lo_scratch", [BATCH, P, HEADS * TOK], F16, kind="Internal").ap()
    o_dram = nc.dram_tensor("o_scratch", [BATCH, P, HEADS * TOK], F32, kind="Internal").ap()
    with ExitStack() as ctx:
        ctx_parts = [ctx.enter_context(nc.sbuf_tensor(n, [P, KC, KEYS + pad], dt))
                     for n, dt, pad in (("ctx_f", F32, 0), ("ctx_h", F16, 3), ("ctx_l", F16, 3))]
        kv_parts = [ctx.enter_context(nc.sbuf_tensor(n, [P, 2, KC, KV_HEADS * HD], F16)) for n in ("w_h", "w_l")]
        q_stored = [ctx.enter_context(nc.semaphore(f"q_stored{i}")) for i in range(2)]
        queries(nc, x, wqT, norm_w, q_hi, q_lo, (wkT, wvT), ctxT, kv_parts, ctx_parts, q_stored)
        cross_attention(nc, ctxT, maskT, kv_parts, ctx_parts, q_hi, q_lo, q_stored, o_dram)
    with nc.sbuf_tensor("x1", [P, TT, HID], F32) as x1:
        output_projection(nc, x, woT, o_dram, x1)
        state_space(nc, winG, wdtT, woutG, params, heads_par, x1)
        experts(nc, raT, bwT, out, x1)


def kernel(**inputs):
    import numpy as np
    import concourse.bacc as bacc
    from concourse.bass_utils import run_bass_kernel_spmd

    a = {n: np.asarray(v) for n, v in inputs.items()}
    win = a["L0_attn_in_proj_w"].T
    conv_dim = INNER + 2 * GROUPS * P

    def group_columns(g):
        gw = GCH * P
        return [win[:, INNER + g * gw:INNER + (g + 1) * gw],
                win[:, 2 * INNER + g * P:2 * INNER + (g + 1) * P],
                win[:, 2 * INNER + GROUPS * P + g * P:2 * INNER + GROUPS * P + (g + 1) * P],
                win[:, g * gw:(g + 1) * gw]]

    def conv_rows(v, g):
        gw = GCH * P
        rows = np.concatenate([v[g * gw:(g + 1) * gw], v[INNER + g * P:INNER + (g + 1) * P],
                               v[INNER + GROUPS * P + g * P:INNER + GROUPS * P + (g + 1) * P]])
        return rows.reshape((CONV, P) + v.shape[1:]).swapaxes(0, 1)

    def channels(v, g):
        return v[g * GCH * P:(g + 1) * GCH * P].reshape(GCH, P).T

    d_rows = np.repeat(a["L0_attn_D"], SSM_P)
    params = np.stack([np.concatenate([conv_rows(a["L0_attn_conv_weight"], g).reshape(P, CONV * TAPS),
                                       conv_rows(a["L0_attn_conv_bias"], g), channels(d_rows, g),
                                       channels(a["L0_attn_norm_weight"], g)], axis=1) for g in range(GROUPS)])
    data = {
        "x": a["x"].reshape(ND, HID),
        "ctxT": a["ctx_4096"].transpose(0, 2, 1),
        "maskT": a["mask_1x1xSxS2_ff0"].reshape(TOK, KEYS).T,
        "wqT": a["L0_xattn_q_proj_w"].T,
        "wkT": a["L0_xattn_k_proj_w"].T,
        "wvT": a["L0_xattn_v_proj_w"].T,
        "woT": a["L0_xattn_o_proj_w"].T,
        "norm_w": np.stack([a["L0_xattn_q_norm_w"], a["L0_xattn_k_norm_w"]], axis=1),
        "winG": np.stack([np.concatenate(group_columns(g), axis=1) for g in range(GROUPS)]),
        "wdtT": win[:, INNER + conv_dim:],
        "woutG": a["L0_attn_out_proj_w"].T.reshape(GROUPS, GCH * P, HID),
        "params": params,
        "heads_par": np.ascontiguousarray(np.broadcast_to(np.stack([a["L0_attn_dt_bias"], a["L0_attn_A_log"]]), (P, 2, SSM_HEADS))),
        "raT": np.concatenate([a["L0_ffn_route_w"], a["L0_ffn_A"].reshape(EXPERTS * RANK, HID)]).T,
        "bwT": a["L0_ffn_Bw"].transpose(0, 2, 1).reshape(EXPERTS * RANK, HID),
    }
    nc = bacc.Bacc("TRN2", target_bir_lowering=False, num_devices=1)
    arrays, args = {}, {}
    for name, v in data.items():
        arrays[name + "_dram"] = np.ascontiguousarray(v)
        args[name] = nc.dram_tensor(name + "_dram", v.shape, F32, kind="ExternalInput").ap()
    out = nc.dram_tensor("out_dram", (ND, HID), F32, kind="ExternalOutput").ap()
    perceiver_block(nc, out=out, **args)
    r = run_bass_kernel_spmd(nc, [arrays], core_ids=[0])
    return r.results[0]["out_dram"].reshape(BATCH, TOK, HID)
```

```python
import concourse.bass as bass
from concourse import mybir
from contextlib import ExitStack

F32 = mybir.dt.float32
F16 = mybir.dt.float16
ALU = mybir.AluOpType
ACT = mybir.ActivationFunctionType
AX = mybir.AxisListType

P = 128
BATCH, TOK, HID = 8, 64, 512
KEYS = 1601
KC = HID // P
HEADS, KV_HEADS, HD = 32, 8, 128
REP = HEADS // KV_HEADS
QC = REP * TOK
KT = -(-KEYS // P)
TAIL = KEYS - (KT - 1) * P
KPAD = KT * P
CH = [(0, 400), (400, 400), (800, 400), (1200, KEYS - 1200)]
NCH = len(CH)
EPS = 1e-5
NEG = -3.0e38

S_CTX, S_W = 16.0, 64.0
S_Q = 64.0
S_KV = 16.0
S_SQ = 2.0
P_LN = 6.931471805599453


STEP_ORDER = ["S0 S1 K0 S2 S3 K1 N S4 V0 S5 K2 S6 M K3 V1 D V2 V3",
              "S0 S1 K0 S2 S3 K1 N S4 V0 S5 K2 S6 M K3 V1 C0 D V2 C1 V3",
              "S0 C2 S1 K0 S2 C3 N S3 K1 S4 S5 K2 S6 M K3 V0 D V1 V2",
              "S0 S1 S2 S3 S4 S5 S6 N M D"]


def wait(eng, sem, value):
    if isinstance(value, int) and value <= 0:
        return
    eng.wait_ge(sem, value)


def row(ap, i):
    if isinstance(i, int):
        return ap[i]
    return ap[bass.ds(i, 1)].rearrange("o p n -> (o p) n")


def cross_attention(nc, ctxT, maskT, kv_parts, ctx_parts, q_hi, q_lo, q_stored, o_dram, NB=BATCH):
    with ExitStack() as ctx:
        def sb(name, shape, dt):
            return ctx.enter_context(nc.sbuf_tensor(name, shape, dt))

        def pb(name, shape):
            return ctx.enter_context(nc.psum_tensor(name, shape, F32))

        def sem(name):
            return ctx.enter_context(nc.semaphore(name))

        U = KV_HEADS
        ctx_f, ctx_h, ctx_l = ctx_parts
        w_h, w_l = kv_parts
        k_h = sb("k_h", [P, 2, KPAD], F16)
        k_l = sb("k_l", [P, 2, KPAD], F16)
        sq_f = sb("sq_f", [P, 2, CH[-1][1] + 3], F32)
        sq_h = sb("sq_h", [P, KPAD], F16)
        sq_l = sb("sq_l", [P, KPAD], F16)
        v_h = sb("v_h", [P, 2, KT, 2 * HD], F16)
        v_l = sb("v_l", [P, 2, KT, 2 * HD], F16)
        S = sb("S", [P, 2, KT, QC], F32)
        p_h = sb("p_h", [P, 2, KT, QC], F16)
        p_l = sb("p_l", [P, 2, KT, QC], F16)
        mask = sb("mask", [P, KT, TOK], F32)
        qh = sb("qh", [P, U, QC], F16)
        ql = sb("ql", [P, U, QC], F16)
        o_st = sb("o_st", [P, U, QC], F32)
        mx = sb("mx", [P, QC], F32)
        mb = sb("mb", [P, QC], F32)
        psum_p = sb("psum_p", [P, 2, QC], F32)
        z = sb("z", [P, 2, 16], F32)
        rk = sb("rk", [P, 2, 16], F32)
        half = sb("half", [P, 16], F32)
        lnb = sb("lnb", [P, 1], F32)
        ones = sb("ones", [P, P], F32)
        one_h = sb("one_h", [P, 1], F16)

        pF = [pb(f"pF{i}", [P, 512]) for i in range(3)]
        pS = [pb(f"pS{i}", [P, 2, QC]) for i in range(2)]
        pO = [pb(f"pO{i}", [P, 2, QC]) for i in range(2)]
        pQ = pb("pQ", [P, 16])

        consts = sem("consts")
        mask_in = sem("mask_in")
        ctx_in = [sem(f"ctx_in{n}") for n in range(NCH)]
        ctx_hi = sem("ctx_hi")
        ctx_lo = sem("ctx_lo")
        q_in = [sem(f"q_in{s}") for s in range(U)]
        proj = sem("proj")
        fill_hi = sem("fill_hi")
        fill_lo = sem("fill_lo")
        sqh_ok = sem("sqh_ok")
        sql_ok = sem("sql_ok")
        ss_ok = sem("ss_ok")
        z_ok = sem("z_ok")
        rk_ok = sem("rk_ok")
        s_ok = sem("s_ok")
        s_out = sem("s_out")
        mx_ok = sem("mx_ok")
        mb_ok = sem("mb_ok")
        turn = sem("turn")
        sub_ok = sem("sub_ok")
        ex_ok = sem("ex_ok")
        ph_ok = sem("ph_ok")
        pl_ok = sem("pl_ok")
        tree = sem("tree")
        sum_ok = sem("sum_ok")
        pv_ok = sem("pv_ok")
        den_ok = sem("den_ok")
        rec_ok = sem("rec_ok")
        o_ok = sem("o_ok")
        o_stored = [sem(f"o_stored{h}") for h in range(2)]

        HALF = [(0, 7), (7, KT)]

        VF = -(-KT // 2)

        def v_fills(s):
            return list(range(3, VF)) if s % 2 == 0 else [0, 1, 2]

        def order(s, last):
            vs = v_fills(s)
            text = STEP_ORDER[0 if s < U - 2 else 1 if s == U - 2 and not last else 0 if s < U - 1 else 3 if last else 2]
            seq = []
            for item in text.split():
                i = int(item[1:] or 0)
                if item[0] != "V":
                    seq.append((item[0], i))
                elif i < len(vs):
                    seq.append(("V", vs[i]))
            return seq

        PRO = [("K", n) for n in range(NCH)] + [("V", f) for f in (0, 1, 2)]
        FILLS = U * NCH + U // 2 * VF

        number = {("K", 0, n): n for n in range(NCH)}
        number |= {("V", 0, f): NCH + f for f in (0, 1, 2)}
        at = len(PRO)
        for s in range(U):
            for kind, i in order(s, False):
                if kind == "K":
                    number["K", s + 1, i] = at
                elif kind == "V":
                    number["V", (s + 1) // 2, i] = at
                else:
                    continue
                at += 1
        assert at == len(PRO) + FILLS

        chunk_used = [1 + max(number["K", U - 1, i], number["V", U // 2 - 1, (c0 + w - 1) // (2 * P)])
                      for i, (c0, w) in enumerate(CH)]

        def fill_no(b, kind, job, i):
            return FILLS * b + number[kind, job, i]

        def loop(eng, body):
            body(0)
            if NB > 2:
                with eng.Fori(1, NB - 1) as b:
                    body(b)
            if NB > 1:
                body(NB - 1)

        def before(b, s, n):
            if s >= n:
                return b, s - n
            return None if isinstance(b, int) and b == 0 else (b - 1, s - n + U)

        def is_last(b):
            return isinstance(b, int) and b == NB - 1

        block = ctx.enter_context(nc.Block())

        def low(eng, b, s, h):
            u = U * b + s
            t0, t1 = HALF[h]
            wait(eng, ph_ok, 2 * u + h + 1)
            eng.tensor_tensor(p_l[:, s % 2, t0:t1, :], S[:, s % 2, t0:t1, :], p_h[:, s % 2, t0:t1, :],
                               ALU.subtract).then_inc(pl_ok, 1)

        def total(eng, b, s):
            u = U * b + s
            T = S[:, s % 2, :, :]
            wait(eng, pl_ok, 2 * (u + 1))
            eng.tensor_tensor(T[:, 0:6, :], T[:, 0:6, :], T[:, 6:12, :], ALU.add).then_inc(tree, 1)
            wait(eng, tree, 4 * u + 1)
            eng.tensor_tensor(T[:, 0:3, :], T[:, 0:3, :], T[:, 3:6, :], ALU.add).then_inc(tree, 1)
            wait(eng, tree, 4 * u + 2)
            eng.tensor_tensor(T[:, 0, :], T[:, 0, :], T[:, 1, :], ALU.add).then_inc(tree, 1)
            eng.tensor_tensor(T[:, 2, :], T[:, 2, :], T[:, 12, :], ALU.add).then_inc(tree, 1)
            wait(eng, tree, 4 * u + 4)
            wait(eng, den_ok, u - 1)
            eng.tensor_tensor(psum_p[:, s % 2, :], T[:, 0, :], T[:, 2, :], ALU.add).then_inc(sum_ok, 1)

        @block.sync
        def _(sp):
            sp.wait_ge(consts, 8)
            sp.dma_start(mask[:, 0:KT - 1, :], maskT[0:(KT - 1) * P, :].rearrange("(t p) q -> p t q", p=P)).then_inc(mask_in, 16)
            sp.dma_start(mask[0:TAIL, KT - 1, :], maskT[(KT - 1) * P:KEYS, :]).then_inc(mask_in, 16)

            def load_ctx(b, n):
                c0, w = CH[n]
                src = row(ctxT, b)[:, c0:c0 + w].rearrange("(k p) c -> p k c", p=P)
                sp.dma_start(ctx_f[:, :, c0:c0 + w], src).then_inc(ctx_in[n], 16)

            def load_q(b, s):
                cols = slice(s * QC, (s + 1) * QC)
                sp.dma_start(qh[:, s, :], row(q_hi, b)[:, cols]).then_inc(q_in[s], 16)
                sp.dma_start(ql[:, s, :], row(q_lo, b)[:, cols]).then_inc(q_in[s], 16)

            for stored, groups in zip(q_stored, (HEADS // 8, HEADS // 8 - 1, 1)):
                sp.wait_ge(stored, 32 * groups)
            for s in range(U):
                load_q(0, s)

            def store_o(b, h, after):
                sp.wait_ge(o_ok, after)
                c = slice(h * U // 2 * QC, (h + 1) * U // 2 * QC)
                sp.dma_start(row(o_dram, b)[:, c], o_st[:, 4 * h:4 * h + 4, :].rearrange("p u q -> p (u q)")).then_inc(o_stored[h], 16)

            def body(b):
                last = is_last(b)
                if not last:
                    wait(sp, ctx_lo, NCH * b)
                    for n in range(NCH):
                        load_ctx(b + 1, n)
                for s in range(U):
                    if s == 2 and not (isinstance(b, int) and b == 0):
                        store_o(b - 1, 1, U * b)
                    if s == 6:
                        store_o(b, 0, U * b + 4)
                    if not last:
                        wait(sp, s_ok, 7 * (U * b + s + 1))
                        load_q(b + 1, s)
            loop(sp, body)
            store_o(NB - 1, 1, U * NB)
            for h in range(2):
                sp.wait_ge(o_stored[h], 16 * NB)

        @block.tensor
        def _(pe):
            def split3(out, a, b, cols, first, final):
                for j, (x, y) in enumerate(((a[0], b[0]), (a[0], b[1]), (a[1], b[0]))):
                    mm = pe.matmul(out, x, y, start=first and j == 0, stop=final and j == 2)
                return mm

            def fill(b, kind, job, i):
                n = fill_no(b, kind, job, i)
                wait(pe, fill_lo, n - 2)
                bank = pF[number[kind, job, i] % 3]
                if kind == "K":
                    head = job % U
                    nb = b + job // U
                    c0, w = CH[i]
                    wait(pe, ctx_lo, NCH * (nb - 1) + i + 1)
                    for k in range(KC):
                        cols = slice(head * HD, (head + 1) * HD)
                        mm = split3(bank[:, 0:w],
                                    (w_h[:, 0, k, cols], w_l[:, 0, k, cols]),
                                    (ctx_h[:, k, c0:c0 + w], ctx_l[:, k, c0:c0 + w]), w, k == 0, k == KC - 1)
                else:
                    pair = job % (U // 2)
                    if job in (0, U // 2) and i == 0:
                        wait(pe, ctx_lo, NCH * (b + job // (U // 2)))
                    cols = slice(pair * 2 * HD, (pair + 1) * 2 * HD)
                    for t in range(2 * i, min(2 * i + 2, KT)):
                        m = min(P, KEYS - t * P)
                        for k in range(KC):
                            mm = split3(bank[0:m, (t % 2) * 256:(t % 2) * 256 + 256],
                                        (ctx_h[:, k, t * P:t * P + m], ctx_l[:, k, t * P:t * P + m]),
                                        (w_h[:, 1, k, cols], w_l[:, 1, k, cols]), 256, k == 0, k == KC - 1)
                mm.then_inc(proj, 1)

            def scores(b, s, p):
                u = U * b + s
                m = 7 * u + p
                wait(pe, s_out, m - 1)
                if p == 0:
                    wait(pe, fill_lo, fill_no(b, "K", s, NCH - 1) + 1)
                    wait(pe, q_in[s], 32 * (b + 1))
                bank = pS[(s * 7 + p) % 2]
                for t in range(2 * p, min(2 * p + 2, KT)):
                    kk = slice(t * P, (t + 1) * P)
                    mm = split3(bank[:, t % 2, :], (k_h[:, s % 2, kk], k_l[:, s % 2, kk]),
                                (qh[:, s, :], ql[:, s, :]), QC, True, True)
                mm.then_inc(s_ok, 1)

            def squares(b, s):
                u = U * b + s
                wait(pe, sqh_ok, NCH * (u + 1))
                wait(pe, sql_ok, NCH * (u + 1))
                wait(pe, z_ok, u)
                for t in range(KT):
                    kk = slice(t * P, (t + 1) * P)
                    pe.matmul(pQ[:, t:t + 1], sq_h[:, kk], one_h[:, :], start=True, stop=False)
                    mm = pe.matmul(pQ[:, t:t + 1], sq_l[:, kk], one_h[:, :], start=False, stop=True)
                mm.then_inc(ss_ok, 1)

            def values(b, s):
                u = U * b + s
                wait(pe, fill_lo, fill_no(b, "V", s // 2, VF - 1) + 1)
                wait(pe, o_ok, u - 1)
                bank = pO[s % 2]
                hv = slice((s % 2) * HD, (s % 2) * HD + HD)
                for t in range(KT):
                    for h in range(2):
                        if t == HALF[h][0]:
                            wait(pe, pl_ok, 2 * u + h + 1)
                            wait(pe, ph_ok, 2 * u + h + 1)
                    mm = split3(bank[:, 0, :], (v_h[:, (s // 2) % 2, t, hv], v_l[:, (s // 2) % 2, t, hv]),
                                (p_h[:, s % 2, t, :], p_l[:, s % 2, t, :]), QC, t == 0, t == KT - 1)
                mm.then_inc(pv_ok, 1)

            def denominators(b, s):
                wait(pe, sum_ok, U * b + s + 1)
                pe.matmul(pO[s % 2][:, 1, :], ones[:, :], psum_p[:, s % 2, :], start=True, stop=True).then_inc(den_ok, 1)

            for kind, i in PRO:
                fill(0, kind, 0, i)
            pe.wait_ge(consts, 8)
            squares(0, 0)

            def body(b):
                last = is_last(b)
                for s in range(U):
                    for kind, i in order(s, last):
                        if kind == "S":
                            scores(b, s, i)
                        elif kind == "K":
                            fill(b, kind, s + 1, i)
                        elif kind == "V":
                            fill(b, kind, (s + 1) // 2, i)
                        elif kind == "N" and before(b, s, 2):
                            denominators(*before(b, s, 2))
                    if not (last and s == U - 1):
                        squares(b, s + 1)
                    if s > 0:
                        values(b, s - 1)
                    elif not (isinstance(b, int) and b == 0):
                        values(b - 1, U - 1)
            loop(pe, body)
            denominators(NB - 1, U - 2)
            values(NB - 1, U - 1)
            denominators(NB - 1, U - 1)

        @block.scalar
        def _(act):
            def ctx_split(b, n):
                c0, w = CH[n]
                act.wait_ge(ctx_in[n], 16 * b)
                act.activation(ctx_h[:, :, c0:c0 + w], ctx_f[:, :, c0:c0 + w], ACT.Copy, scale=S_CTX).then_inc(ctx_hi, 1)

            def fill(b, kind, job, i):
                n = fill_no(b, kind, job, i)
                wait(act, proj, n + 1)
                bank = pF[number[kind, job, i] % 3]
                if kind == "K":
                    u = U * b + job
                    c0, w = CH[i]
                    c = NCH * u + i
                    if i == 0:
                        wait(act, s_ok, 7 * (u - 1))
                    act.activation(k_h[:, job % 2, c0:c0 + w], bank[:, 0:w], ACT.Copy, scale=S_KV / (S_CTX * S_W))
                    wait(act, sql_ok, c - 1)
                    act.activation(sq_f[:, i % 2, 0:w], bank[:, 0:w], ACT.Square, scale=S_SQ / (S_CTX * S_W)).then_inc(fill_hi, 1)
                    if i == 0:
                        wait(act, ss_ok, u)
                    act.wait_ge(fill_hi, n + 1)
                    act.activation(sq_h[:, c0:c0 + w], sq_f[:, i % 2, 0:w], ACT.Copy).then_inc(sqh_ok, 1)
                else:
                    if i == 0:
                        wait(act, pv_ok, U * b + 2 * job - 2)
                    tiles = min(2, KT - 2 * i)
                    m = P if tiles == 2 else TAIL
                    act.activation(v_h[0:m, job % 2, 2 * i:2 * i + tiles, :],
                                   bank[0:m, 0:256 * tiles].rearrange("p (t c) -> p t c", c=256),
                                   ACT.Copy, scale=S_KV / (S_CTX * S_W)).then_inc(fill_hi, 1)

            def probabilities(b, s, h):
                u = U * b + s
                t0, t1 = HALF[h]
                act.wait_ge(sub_ok, 2 * u + h + 1)
                act.activation(S[:, s % 2, t0:t1, :], S[:, s % 2, t0:t1, :], ACT.Exp, bias=lnb[:, 0:1]).then_inc(ex_ok, 1)
                wait(act, pv_ok, u - 1)
                act.wait_ge(ex_ok, 2 * u + h + 1)
                act.activation(p_h[:, s % 2, t0:t1, :], S[:, s % 2, t0:t1, :], ACT.Copy).then_inc(ph_ok, 1)

            act.wait_ge(consts, 8)
            for kind, i in PRO:
                fill(0, kind, 0, i)

            def body(b):
                last = is_last(b)
                first = isinstance(b, int) and b == 0
                for s in range(U):
                    prev = (b, s - 1) if s else (b - 1, U - 1)
                    if not (first and s == 0):
                        probabilities(*prev, 0)
                    done = first and s == 0
                    for kind, i in order(s, last):
                        if kind in "KV":
                            fill(b, kind, s + 1 if kind == "K" else (s + 1) // 2, i)
                            if not done:
                                probabilities(*prev, 1)
                                done = True
                        elif kind == "C":
                            wait(act, proj, FILLS * b + chunk_used[i])
                            ctx_split(b + 1, i)
                    if not done:
                        probabilities(*prev, 1)
            loop(act, body)
            for h in range(2):
                probabilities(NB - 1, U - 1, h)

        @block.vector
        def _(dve):
            dve.memset(k_h[:, :, KEYS:KPAD], 0.0).then_inc(consts, 1)
            dve.memset(k_l[:, :, KEYS:KPAD], 0.0).then_inc(consts, 1)
            dve.memset(sq_h[:, KEYS:KPAD], 0.0).then_inc(consts, 1)
            dve.memset(sq_l[:, KEYS:KPAD], 0.0).then_inc(consts, 1)
            dve.memset(one_h[:, :], 1.0)
            dve.memset(half[:, :], -0.5)
            dve.memset(lnb[:, :], P_LN)
            dve.memset(ones[:, :], 1.0).then_inc(consts, 1)
            dve.memset(mask[:, KT - 1, :], NEG).then_inc(consts, 1)
            dve.memset(v_h[:, :, KT - 1, :], 0.0).then_inc(consts, 1)
            dve.memset(v_l[:, :, KT - 1, :], 0.0).then_inc(consts, 1)
            def ctx_split(b, n):
                c0, w = CH[n]
                dve.wait_ge(ctx_hi, NCH * (b - 1) + n + 1)
                dve.scalar_tensor_tensor(out=ctx_l[:, :, c0:c0 + w], in0=ctx_f[:, :, c0:c0 + w], scalar=S_CTX,
                                         in1=ctx_h[:, :, c0:c0 + w], op0=ALU.mult, op1=ALU.subtract).then_inc(ctx_lo, 1)

            def fill(b, kind, job, i):
                n = fill_no(b, kind, job, i)
                dve.wait_ge(fill_hi, n + 1)
                bank = pF[number[kind, job, i] % 3]
                if kind == "K":
                    c0, w = CH[i]
                    c = NCH * (U * b + job) + i
                    dve.scalar_tensor_tensor(out=k_l[:, job % 2, c0:c0 + w], in0=bank[:, 0:w], scalar=S_KV / (S_CTX * S_W),
                                             in1=k_h[:, job % 2, c0:c0 + w], op0=ALU.mult, op1=ALU.subtract).then_inc(fill_lo, 1)
                    dve.wait_ge(sqh_ok, c + 1)
                    dve.tensor_tensor(sq_l[:, c0:c0 + w], sq_f[:, i % 2, 0:w], sq_h[:, c0:c0 + w], ALU.subtract).then_inc(sql_ok, 1)
                else:
                    tiles = min(2, KT - 2 * i)
                    m = P if tiles == 2 else TAIL
                    vv = v_h[0:m, job % 2, 2 * i:2 * i + tiles, :]
                    dve.scalar_tensor_tensor(out=v_l[0:m, job % 2, 2 * i:2 * i + tiles, :],
                                             in0=bank[0:m, 0:256 * tiles].rearrange("p (t c) -> p t c", c=256),
                                             scalar=S_KV / (S_CTX * S_W), in1=vv, op0=ALU.mult, op1=ALU.subtract).then_inc(fill_lo, 1)

            def norms(b, s):
                u = U * b + s
                wait(dve, ss_ok, u + 1)
                scale2 = (S_KV * S_Q) ** 2 * HD
                dve.tensor_scalar(z[:, s % 2, 0:KT], pQ[:, 0:KT], scale2 / (HD * S_SQ ** 2), scale2 * EPS,
                                  ALU.mult, ALU.add).then_inc(z_ok, 1)

            def evacuate(b, s, p):
                u = U * b + s
                if p == 0:
                    wait(dve, rk_ok, u + 1)
                    wait(dve, sum_ok, u - 1)
                wait(dve, s_ok, 7 * u + p + 1)
                bank = pS[(s * 7 + p) % 2]
                for t in range(2 * p, min(2 * p + 2, KT)):
                    ins = dve.scalar_tensor_tensor(
                        out=S[:, s % 2, t, :].rearrange("p (r q) -> p r q", r=REP),
                        in0=bank[:, t % 2, :].rearrange("p (r q) -> p r q", r=REP),
                        scalar=rk[:, s % 2, t:t + 1], in1=mask[:, t, :].unsqueeze(1).to_broadcast([P, REP, TOK]),
                        op0=ALU.mult, op1=ALU.add)
                ins.then_inc(s_out, 1)

            def maximum(b, s):
                u = U * b + s
                wait(dve, s_out, 7 * (u + 1))
                dve.tensor_reduce(mx[:, :], S[:, s % 2, :, :].rearrange("p t q -> p q t"), AX.X, ALU.max).then_inc(mx_ok, 1)

            def subtract(b, s, h):
                u = U * b + s
                if h == 0:
                    wait(dve, mb_ok, u + 1)
                t0, t1 = HALF[h]
                v = S[:, s % 2, t0:t1, :]
                dve.tensor_tensor(v, v, mb[:, :].unsqueeze(1).to_broadcast([P, t1 - t0, QC]), ALU.subtract).then_inc(sub_ok, 1)

            def output(b, s):
                u = U * b + s
                wait(dve, den_ok, u + 1)
                bank = pO[s % 2]
                if s % 4 == 0:
                    wait(dve, o_stored[s // 4], 16 * b)
                dve.reciprocal(o_st[:, s, :], bank[:, 1, :]).then_inc(rec_ok, 1)
                dve.wait_ge(rec_ok, u + 1)
                dve.scalar_tensor_tensor(out=o_st[:, s, :], in0=bank[:, 0, :], scalar=1.0 / S_KV, in1=o_st[:, s, :],
                                         op0=ALU.mult, op1=ALU.mult).then_inc(o_ok, 1)

            for kind, i in PRO:
                fill(0, kind, 0, i)
            norms(0, 0)
            dve.wait_ge(mask_in, 32)

            def body(b):
                last = is_last(b)
                first = isinstance(b, int) and b == 0
                for s in range(U):
                    for kind, i in order(s, last):
                        if kind == "S":
                            evacuate(b, s, i)
                        elif kind in "KV":
                            fill(b, kind, s + 1 if kind == "K" else (s + 1) // 2, i)
                        elif kind == "C":
                            ctx_split(b + 1, i)
                        elif kind == "M":
                            maximum(b, s)
                        elif kind == "D":
                            subtract(b, s, 0)
                            subtract(b, s, 1)
                        elif kind == "N" and before(b, s, 2):
                            output(*before(b, s, 2))
                    if not (last and s == U - 1):
                        norms(b, s + 1)
            loop(dve, body)
            for h in range(2):
                low(dve, NB - 1, U - 1, h)
            output(NB - 1, U - 2)
            total(dve, NB - 1, U - 1)
            output(NB - 1, U - 1)

        @block.gpsimd
        def _(pool):
            def power(b, s):
                u = U * b + s
                wait(pool, z_ok, u + 1)
                wait(pool, s_out, 7 * (u - 1))
                pool.tensor_tensor(rk[:, s % 2, 0:KT], z[:, s % 2, 0:KT], half[:, 0:KT], ALU.pow).then_inc(rk_ok, 1)

            def reduce(b, s):
                u = U * b + s
                wait(pool, mx_ok, u + 1)
                pool.sem_inc(turn, 1)
                pool.partition_all_reduce(mb[:, :], mx[:, :], P, bass.bass_isa.ReduceOp.max).then_inc(mb_ok, 1)

            pool.wait_ge(consts, 8)
            power(0, 0)

            def body(b):
                last = is_last(b)
                first = isinstance(b, int) and b == 0
                for s in range(U):
                    prev = (b, s - 1) if s else (b - 1, U - 1)
                    have = not (first and s == 0)
                    if have:
                        low(pool, *prev, 0)
                        low(pool, *prev, 1)
                        total(pool, *prev)
                    reduce(b, s)
                    if not (last and s == U - 1):
                        power(b, s + 1)
            loop(pool, body)
S_H = 16.0
S_O = 64.0
S_Y = 16.0
GROUPS = 8
TT = BATCH * TOK // P
ND = BATCH * TOK
INNER = 4096
GCH = INNER // GROUPS // P
CONV = GCH + 2
TAPS = 4
SSM_HEADS, SSM_P = 64, 64
GH = SSM_HEADS // GROUPS
NIN = CONV + GCH
CW = CONV * P
NPAR = CONV * TAPS + CONV + 2 * GCH
EXPERTS, RANK = 8, 16


def split3(pe, out, a, b, first, final):
    for j, (x, y) in enumerate(((a[0], b[0]), (a[0], b[1]), (a[1], b[0]))):
        mm = pe.matmul(out, x, y, start=first and j == 0, stop=final and j == 2)
    return mm


class LayerNorm:

    def __init__(self, nc, ctx, tag, x, ident, eps, banks, out):
        self.nc, self.x, self.ident, self.eps, self.banks, self.out = nc, x, ident, eps, banks, out
        self.st = ctx.enter_context(nc.sbuf_tensor(f"{tag}_st", [P, TT, 6], F32))
        self.mv = ctx.enter_context(nc.sbuf_tensor(f"{tag}_mv", [P, TT, 2], F32))
        self.sd = ctx.enter_context(nc.sbuf_tensor(f"{tag}_sd", [P, TT], F32))
        self.rs = ctx.enter_context(nc.sbuf_tensor(f"{tag}_rs", [P, TT], F32))
        self.xn = ctx.enter_context(nc.sbuf_tensor(f"{tag}_xn", [P, TT, HID], F32))
        self.moments, self.std, self.rstd, self.normed, self.turned, self.done = [
            ctx.enter_context(nc.semaphore(f"{tag}_{name}"))
            for name in "moments std rstd normed turned done".split()]
        if len(out) == 2:
            self.high = ctx.enter_context(nc.semaphore(f"{tag}_high"))

    def vector(self, dve):
        for t in range(TT):
            dve.bn_stats(self.st[:, t, :], self.x[:, t, :]).then_inc(self.moments, 1)
        for t in range(TT):
            dve.wait_ge(self.moments, TT)
            dve.bn_aggr(self.mv[:, t, :], self.st[:, t, :]).then_inc(self.moments, 1)
        dve.wait_ge(self.std, 1)
        dve.reciprocal(self.rs[:, :], self.sd[:, :]).then_inc(self.rstd, 1)
        dve.wait_ge(self.rstd, 1)
        for t in range(TT):
            dve.tensor_scalar(self.xn[:, t, :], self.x[:, t, :], self.mv[:, t, 0:1], self.rs[:, t:t + 1],
                              ALU.subtract, ALU.mult).then_inc(self.normed, 1)
    def vector_turned(self, dve):
        for t in range(TT):
            bank = self.banks[t % 2]
            cols = slice(t * P, (t + 1) * P)
            if len(self.out) == 1:
                dve.wait_ge(self.turned, t + 1)
                dve.tensor_copy(self.out[0][:, :, cols], bank[:, :].rearrange("p (k c) -> p k c", k=KC)).then_inc(self.done, 1)
            else:
                th, tl = self.out
                dve.wait_ge(self.high, t + 1)
                dve.scalar_tensor_tensor(out=tl[:, :, cols], in0=bank[:, :].rearrange("p (k c) -> p k c", k=KC), scalar=S_H,
                                         in1=th[:, :, cols], op0=ALU.mult, op1=ALU.subtract).then_inc(self.done, 1)

    def scalar(self, act):
        act.wait_ge(self.moments, 2 * TT)
        act.activation(self.sd[:, :], self.mv[:, :, 1], ACT.Sqrt, bias=self.eps).then_inc(self.std, 1)
    def scalar_turned(self, act):
        if len(self.out) == 2:
            for t in range(TT):
                act.wait_ge(self.turned, t + 1)
                act.activation(self.out[0][:, :, t * P:(t + 1) * P], self.banks[t % 2][:, :].rearrange("p (k c) -> p k c", k=KC),
                               ACT.Copy, scale=S_H).then_inc(self.high, 1)

    def tensor(self, pe):
        for t in range(TT):
            pe.wait_ge(self.normed, t + 1)
            wait(pe, self.done, t - 1)
            for k in range(KC):
                mm = pe.transpose(self.banks[t % 2][:, k * P:(k + 1) * P], self.xn[:, t, k * P:(k + 1) * P], self.ident)
            mm.then_inc(self.turned, 1)


def identity(pool, ident, sem):
    pool.memset(ident, 0.0).then_inc(sem, 1)
    pool.wait_ge(sem, 1)
    pool.affine_select(out=ident, in_=ident, compare_op=ALU.not_equal, fill=1.0, base=0,
                       pattern=[[-1, P]], channel_multiplier=1).then_inc(sem, 1)


def queries(nc, x, wqT, norm_w, q_hi, q_lo, kvT, ctxT, kv_parts, ctx_parts, stored):
    with ExitStack() as ctx:
        def sb(name, shape, dt):
            return ctx.enter_context(nc.sbuf_tensor(name, shape, dt))

        def sem(name):
            return ctx.enter_context(nc.semaphore(name))

        GR = HEADS // 4
        xs = sb("q_x", [P, TT, HID], F32)
        ident = sb("q_ident", [P, P], F32)
        eps = sb("q_eps", [P, 1], F32)
        eps2 = sb("q_eps2", [P, 1], F32)
        nw = sb("q_nw", [P, 2], F32)
        nwp = sb("q_nwp", [P, 1], F32)
        th = sb("q_th", [P, KC, ND], F16)
        tl = sb("q_tl", [P, KC, ND], F16)
        wst = sb("q_wst", [P, 2, KC, 512], F32)
        wh = sb("q_wh", [P, 2, KC, 512], F16)
        wl = sb("q_wl", [P, 2, KC, 512], F16)
        sq = sb("q_sq", [P, 2, 512], F32)
        ss = sb("q_ss", [P, 2, 4], F32)
        sd = sb("q_sd", [P, 2, 4], F32)
        rs = sb("q_rs", [P, 2, 4], F32)
        qs = sb("q_qs", [P, TT, 512], F32)
        kvst = sb("q_kvst", [P, 2, KC, 512], F32)
        kv_h, kv_l = kv_parts
        ctx_f, ctx_h, ctx_l = ctx_parts
        qh = sb("q_qh", [P, 2, BATCH, 4 * TOK], F16)
        ql = sb("q_ql", [P, 2, BATCH, 4 * TOK], F16)
        pT = [ctx.enter_context(nc.psum_tensor(f"q_pT{i}", [P, 512], F32)) for i in range(2)]
        pQ = [ctx.enter_context(nc.psum_tensor(f"q_pQ{i}", [P, 512], F32)) for i in range(TT)]
        pR = [ctx.enter_context(nc.psum_tensor(f"q_pR{i}", [P, 512], F32)) for i in range(2)]

        x_in = sem("q_x_in")
        nw_in = sem("q_nw_in")
        consts = sem("q_consts")
        idt = sem("q_idt")
        w_in = [sem(f"q_w_in{i}") for i in range(2)]
        w_hi = sem("q_w_hi")
        w_lo = sem("q_w_lo")
        q_ok = sem("q_q_ok")
        sq_ok = sem("q_sq_ok")
        ss_ok = sem("q_ss_ok")
        sd_ok = sem("q_sd_ok")
        rs_ok = sem("q_rs_ok")
        qs_ok = sem("q_qs_ok")
        t_ok = sem("q_t_ok")
        hi_ok = sem("q_hi_ok")
        lo_ok = sem("q_lo_ok")
        kv_in = [sem(f"q_kv_in{i}") for i in range(2)]
        kv_hi = sem("q_kv_hi")
        kv_lo = sem("q_kv_lo")
        ctx_in = [sem(f"q_ctx_in{n}") for n in range(NCH)]
        ctx_hi = sem("q_ctx_hi")
        ctx_lo = sem("q_ctx_lo")
        ln = LayerNorm(nc, ctx, "qln", xs, ident[:, :], eps[:, 0:1], pT, (th, tl))
        block = ctx.enter_context(nc.Block())

        def loop(eng, body):
            for j in range(2):
                body(0, j)
            with eng.Fori(1, GR // 2 - 1) as pair:
                for j in range(2):
                    body(pair, j)
            for j in range(2):
                body(GR // 2 - 1, j)

        LAG = 2

        def earlier(pair, j, t):
            if t >= LAG:
                return pair, j, t - LAG
            if j:
                return pair, 0, t - LAG + TT
            return None if isinstance(pair, int) and pair == 0 else (pair - 1, 1, t - LAG + TT)

        def gap_jobs(pair, j, t):
            if not isinstance(pair, int):
                return []
            if pair == 0:
                return [("W", j)] if t == 3 else []
            return [[("W", 2)], [], [("W", 3)], [("C", 0)], [], [("C", 1)], [("C", 2)], [("C", 3)]][4 * j + t]

        def store(eng, pair, j, signal):
            g = 2 * pair + j
            wait(eng, lo_ok, TT * (g + 1))
            for dram, st in ((q_hi, qh), (q_lo, ql)):
                dst = dram[:, :, g * 256:(g + 1) * 256] if isinstance(g, int) else dram[:, :, bass.ds(g * 256, 256)]
                eng.dma_start(dst.rearrange("b p c -> p b c"), st[:, j, :, :]).then_inc(signal, 16)

        @block.sync
        def _(sp):
            sp.dma_start(xs[:, :, :], x.rearrange("(t p) c -> p t c", p=P)).then_inc(x_in, 16)
            sp.dma_start(nw[:, :], norm_w).then_inc(nw_in, 16)

            def body(pair, j):
                g = 2 * pair + j
                wait(sp, w_lo, g - 1)
                src = wqT[:, g * 512:(g + 1) * 512] if isinstance(g, int) else wqT[:, bass.ds(g * 512, 512)]
                sp.dma_start(wst[:, j, :, :], src.rearrange("(k p) c -> p k c", p=P)).then_inc(w_in[j], 16)

            def load_kv(n):
                sp.dma_start(kvst[:, n % 2, :, :], kvT[n // 2][:, 512 * (n % 2):512 * (n % 2) + 512]
                             .rearrange("(k p) c -> p k c", p=P)).then_inc(kv_in[n % 2], 16)

            for j in range(2):
                body(0, j)
            for n in range(2):
                load_kv(n)
            for n, (c0, w) in enumerate(CH):
                sp.dma_start(ctx_f[:, :, c0:c0 + w], ctxT[0][:, c0:c0 + w].rearrange("(k p) c -> p k c", p=P)).then_inc(ctx_in[n], 16)
            with sp.Fori(1, GR // 2 - 1) as pair:
                for j in range(2):
                    body(pair, j)
            for n in range(2):
                sp.wait_ge(kv_lo, n + 1)
                load_kv(2 + n)
            for j in range(2):
                body(GR // 2 - 1, j)
            store(sp, GR // 2 - 1, 1, stored[2])

        @block.gpsimd
        def _(pool):
            identity(pool, ident[:, :], idt)

            def body(pair, j):
                if not (isinstance(pair, int) and pair == GR // 2 - 1 and j == 1):
                    store(pool, pair, j, stored[j])
            loop(pool, body)

        @block.tensor
        def _(pe):
            pe.wait_ge(idt, 2)
            ln.tensor(pe)
            pe.wait_ge(ln.done, TT)

            def turn(pair, j, t):
                n = TT * (2 * pair + j) + t
                wait(pe, qs_ok, n + 1)
                wait(pe, lo_ok, n - 1)
                for h in range(4):
                    mm = pe.transpose(pR[t % 2][:, h * P:(h + 1) * P], qs[:, t, h * P:(h + 1) * P], ident[:, :])
                mm.then_inc(t_ok, 1)

            def body(pair, j):
                g = 2 * pair + j
                wait(pe, w_lo, g + 1)
                for t in range(TT):
                    n = TT * g + t
                    wait(pe, qs_ok, n - TT + 1)
                    for k in range(KC):
                        mm = split3(pe, pQ[t][:, :], (th[:, k, t * P:(t + 1) * P], tl[:, k, t * P:(t + 1) * P]),
                                    (wh[:, j, k, :], wl[:, j, k, :]), k == 0, k == KC - 1)
                    mm.then_inc(q_ok, 1)
                    if earlier(pair, j, t):
                        turn(*earlier(pair, j, t))
            loop(pe, body)
            for t in range(TT - LAG, TT):
                turn(GR // 2 - 1, 1, t)

        @block.scalar
        def _(act):
            def high(pair, j, t):
                n = TT * (2 * pair + j) + t
                if t == 0:
                    wait(act, stored[j], 32 * pair)
                wait(act, t_ok, n + 1)
                if isinstance(pair, int) and pair == 0 and j == 0 and t == 0:
                    act.wait_ge(consts, 3)
                out = qh[:, j, 2 * t:2 * t + 2, :].rearrange("p b (h q) -> p h b q", h=4)
                act.activation(out, pR[t % 2][:, :].rearrange("p (h b q) -> p h b q", h=4, b=2), ACT.Copy,
                               scale=nwp[:, 0:1]).then_inc(hi_ok, 1)

            def split(pair, j):
                g = 2 * pair + j
                wait(act, w_in[j], 16 * (pair + 1))
                wait(act, q_ok, TT * (g - 1))
                act.activation(wh[:, j, :, :], wst[:, j, :, :], ACT.Copy, scale=S_W).then_inc(w_hi, 1)

            def gap_split(kind, n):
                if kind == "W":
                    act.wait_ge(kv_in[n % 2], 16 * (n // 2 + 1))
                    act.activation(kv_h[:, n // 2, :, 512 * (n % 2):512 * (n % 2) + 512], kvst[:, n % 2, :, :],
                                   ACT.Copy, scale=S_W).then_inc(kv_hi, 1)
                else:
                    c0, w = CH[n]
                    act.wait_ge(ctx_in[n], 16)
                    act.activation(ctx_h[:, :, c0:c0 + w], ctx_f[:, :, c0:c0 + w], ACT.Copy, scale=S_CTX).then_inc(ctx_hi, 1)

            act.wait_ge(consts, 2)
            ln.scalar(act)
            split(0, 0)
            ln.scalar_turned(act)

            def body(pair, j):
                g = 2 * pair + j
                for t in range(TT):
                    if t == 2 and not (isinstance(g, int) and g == GR - 1):
                        split(pair + j, 1 - j)
                    n = TT * g + t
                    wait(act, q_ok, n + 1)
                    wait(act, ss_ok, n - 1)
                    act.activation(sq[:, t % 2, :], pQ[t][:, :], ACT.Square, scale=1.0 / (S_H * S_W)).then_inc(sq_ok, 1)
                    wait(act, ss_ok, n + 1)
                    wait(act, rs_ok, n - 1)
                    act.activation(sd[:, t % 2, :], ss[:, t % 2, :], ACT.Sqrt, bias=eps2[:, 0:1],
                                   scale=(S_H * S_W / S_Q) ** 2 / HD).then_inc(sd_ok, 1)
                    if earlier(pair, j, t):
                        high(*earlier(pair, j, t))
                    for job in gap_jobs(pair, j, t):
                        gap_split(*job)
            loop(act, body)
            for t in range(TT - LAG, TT):
                high(GR // 2 - 1, 1, t)

        @block.vector
        def _(dve):
            dve.memset(eps[:, :], EPS).then_inc(consts, 1)
            dve.memset(eps2[:, :], EPS * (S_H * S_W / S_Q) ** 2).then_inc(consts, 1)
            dve.wait_ge(nw_in, 16)
            dve.tensor_tensor(nwp[:, :], nw[:, 0:1], nw[:, 1:2], ALU.mult).then_inc(consts, 1)
            dve.wait_ge(x_in, 16)
            ln.vector(dve)

            def split(pair, j):
                wait(dve, w_hi, 2 * pair + j + 1)
                dve.scalar_tensor_tensor(out=wl[:, j, :, :], in0=wst[:, j, :, :], scalar=S_W, in1=wh[:, j, :, :],
                                         op0=ALU.mult, op1=ALU.subtract).then_inc(w_lo, 1)

            def gap_split(kind, n):
                if kind == "W":
                    cols = slice(512 * (n % 2), 512 * (n % 2) + 512)
                    dve.wait_ge(kv_hi, n + 1)
                    dve.scalar_tensor_tensor(out=kv_l[:, n // 2, :, cols], in0=kvst[:, n % 2, :, :], scalar=S_W,
                                             in1=kv_h[:, n // 2, :, cols], op0=ALU.mult, op1=ALU.subtract).then_inc(kv_lo, 1)
                else:
                    c0, w = CH[n]
                    dve.wait_ge(ctx_hi, n + 1)
                    dve.scalar_tensor_tensor(out=ctx_l[:, :, c0:c0 + w], in0=ctx_f[:, :, c0:c0 + w], scalar=S_CTX,
                                             in1=ctx_h[:, :, c0:c0 + w], op0=ALU.mult, op1=ALU.subtract).then_inc(ctx_lo, 1)

            split(0, 0)
            ln.vector_turned(dve)

            def low(pair, j, t):
                n = TT * (2 * pair + j) + t
                wait(dve, hi_ok, n + 1)
                dve.wait_ge(consts, 3)
                out = ql[:, j, 2 * t:2 * t + 2, :].rearrange("p b (h q) -> p b h q", h=4)
                hi = qh[:, j, 2 * t:2 * t + 2, :].rearrange("p b (h q) -> p b h q", h=4)
                src = pR[t % 2][:, :].rearrange("p (h b q) -> p b h q", h=4, b=2)
                for b in range(2):
                    mm = dve.scalar_tensor_tensor(out=out[:, b, :, :], in0=src[:, b, :, :], scalar=nwp[:, 0:1],
                                                  in1=hi[:, b, :, :], op0=ALU.mult, op1=ALU.subtract)
                mm.then_inc(lo_ok, 1)

            def body(pair, j):
                g = 2 * pair + j
                for t in range(TT):
                    n = TT * g + t
                    if t == 2 and not (isinstance(g, int) and g == GR - 1):
                        split(pair + j, 1 - j)
                    wait(dve, sq_ok, n + 1)
                    dve.tensor_reduce(ss[:, t % 2, :], sq[:, t % 2, :].rearrange("p (h c) -> p h c", h=4), AX.X, ALU.add).then_inc(ss_ok, 1)
                    wait(dve, sd_ok, n + 1)
                    dve.reciprocal(rs[:, t % 2, :], sd[:, t % 2, :]).then_inc(rs_ok, 1)
                    wait(dve, rs_ok, n + 1)
                    wait(dve, t_ok, n - TT + 1)
                    dve.tensor_tensor(qs[:, t, :].rearrange("p (h c) -> p h c", h=4),
                                      pQ[t][:, :].rearrange("p (h c) -> p h c", h=4),
                                      rs[:, t % 2, :].unsqueeze(2).to_broadcast([P, 4, HD]), ALU.mult).then_inc(qs_ok, 1)
                    if earlier(pair, j, t):
                        low(*earlier(pair, j, t))
                    for job in gap_jobs(pair, j, t):
                        gap_split(*job)
            loop(dve, body)
            for t in range(TT - LAG, TT):
                low(GR // 2 - 1, 1, t)


def output_projection(nc, start, x, woT, o_dram, x1):
    with ExitStack() as ctx:
        def sb(name, shape, dt):
            return ctx.enter_context(nc.sbuf_tensor(name, shape, dt))

        def sem(name):
            return ctx.enter_context(nc.semaphore(name))

        HS, SLOTS = 2, 4
        GR = HEADS // HS
        GW = HS * TOK
        xs = sb("p_x", [P, TT, HID], F32)
        ost = sb("p_ost", [P, SLOTS, BATCH, GW], F32)
        wst = sb("p_wst", [P, SLOTS, HS, HID], F32)
        oh = sb("p_oh", [P, SLOTS, HS, ND], F16)
        ol = sb("p_ol", [P, SLOTS, HS, ND], F16)
        wh = sb("p_wh", [P, SLOTS, HS, HID], F16)
        wl = sb("p_wl", [P, SLOTS, HS, HID], F16)
        pO = [ctx.enter_context(nc.psum_tensor(f"p_pO{i}", [P, HID], F32)) for i in range(TT)]
        x_in = sem("p_x_in")
        g_in = [sem(f"p_g_in{i}") for i in range(SLOTS)]
        hi = sem("p_hi")
        lo = sem("p_lo")
        made = sem("p_made")
        added = sem("p_added")
        block = ctx.enter_context(nc.Block())

        def loop(eng, body):
            for j in range(SLOTS):
                body(0, j)
            with eng.Fori(1, GR // SLOTS - 1) as turn:
                for j in range(SLOTS):
                    body(turn, j)
            for j in range(SLOTS):
                body(GR // SLOTS - 1, j)

        @block.sync
        def _(sp):
            def body(turn, j):
                g = SLOTS * turn + j
                wait(sp, lo, 2 * (g + 1 - SLOTS))
                if isinstance(g, int):
                    so, sw = o_dram[:, :, g * GW:(g + 1) * GW], woT[g * HS * P:(g + 1) * HS * P, :]
                else:
                    so, sw = o_dram[:, :, bass.ds(g * GW, GW)], woT[bass.ds(g * HS * P, HS * P), :]
                sp.dma_start(ost[:, j, :, :], so.rearrange("b p c -> p b c")).then_inc(g_in[j], 16)
                sp.dma_start(wst[:, j, :, :], sw.rearrange("(h p) c -> p h c", p=P)).then_inc(g_in[j], 16)
            loop(sp, body)
            start.sync(sp)
            sp.dma_start(xs[:, :, :], x.rearrange("(t p) c -> p t c", p=P)).then_inc(x_in, 16)

        @block.scalar
        def _(act):
            def body(turn, j):
                g = SLOTS * turn + j
                wait(act, g_in[j], 32 * (turn + 1))
                wait(act, made, g + 1 - SLOTS)
                act.activation(oh[:, j, :, :].rearrange("p h (b q) -> p h b q", b=BATCH),
                               ost[:, j, :, :].rearrange("p b (h q) -> p h b q", h=HS), ACT.Copy, scale=S_O).then_inc(hi, 1)
                act.activation(wh[:, j, :, :], wst[:, j, :, :], ACT.Copy, scale=S_W).then_inc(hi, 1)
            loop(act, body)
            start.scalar(act)

        @block.vector
        def _(dve):
            def body(turn, j):
                g = SLOTS * turn + j
                wait(dve, hi, 2 * g + 1)
                for h in range(HS):
                    v = ost[:, j, :, :].rearrange("p b (h q) -> p h b q", h=HS)[:, h, :, :]
                    i = dve.scalar_tensor_tensor(out=ol[:, j, h, :].rearrange("p (b q) -> p b q", b=BATCH), in0=v, scalar=S_O,
                                                 in1=oh[:, j, h, :].rearrange("p (b q) -> p b q", b=BATCH),
                                                 op0=ALU.mult, op1=ALU.subtract)
                i.then_inc(lo, 1)
                wait(dve, hi, 2 * g + 2)
                dve.scalar_tensor_tensor(out=wl[:, j, :, :], in0=wst[:, j, :, :], scalar=S_W, in1=wh[:, j, :, :],
                                         op0=ALU.mult, op1=ALU.subtract).then_inc(lo, 1)
            loop(dve, body)
            start.vector(dve)
            dve.wait_ge(x_in, 16)
            dve.wait_ge(made, GR)
            for t in range(TT):
                dve.scalar_tensor_tensor(out=x1[:, t, :], in0=pO[t][:, :], scalar=1.0 / (S_O * S_W), in1=xs[:, t, :],
                                         op0=ALU.mult, op1=ALU.add).then_inc(added, 1)

        @block.gpsimd
        def _(pool):
            start.gpsimd(pool)

        @block.tensor
        def _(pe):
            def body(turn, j):
                g = SLOTS * turn + j
                wait(pe, lo, 2 * (g + 1))
                first = isinstance(g, int) and g == 0
                final = isinstance(g, int) and g == GR - 1
                for t in range(TT):
                    for h in range(HS):
                        mm = split3(pe, pO[t][:, :], (oh[:, j, h, t * P:(t + 1) * P], ol[:, j, h, t * P:(t + 1) * P]),
                                    (wh[:, j, h, :], wl[:, j, h, :]), first and h == 0, final and h == HS - 1)
                mm.then_inc(made, 1)
            loop(pe, body)


class SsmStart:

    def __init__(self, nc, ctx, winG, wdtT, heads_par):
        def sb(name, shape, dt=F32):
            return ctx.enter_context(nc.sbuf_tensor("s_" + name, shape, dt))

        self.winG, self.wdtT, self.heads_par = winG, wdtT, heads_par
        self.ident, self.ones = sb("ident", [P, P]), sb("ones", [P, P])
        self.upto = sb("upto", [P, P])
        self.after = sb("after", [P, P])
        self.eps = sb("eps", [P, 1])
        self.hp = sb("hp", [P, 2, SSM_HEADS])
        self.wst, self.wh, self.wl = [sb(n, [P, KC, NIN * P], dt) for n, dt in (("wst", F32), ("wh", F16), ("wl", F16))]
        self.wdt, self.wdh, self.wdl = [sb(n, [P, KC, SSM_HEADS], dt) for n, dt in (("wdt", F32), ("wdh", F16), ("wdl", F16))]
        (self.idt, self.cst, self.wdt_in, self.hp_in, self.wdt_hi, self.wdt_lo, self.wA_in, self.wA_hi, self.wA_lo,
         self.wB_in, self.wB_hi, self.wB_lo) = [ctx.enter_context(nc.semaphore("s_" + n)) for n in (
             "idt cst wdt_in hp_in wdt_hi wdt_lo wA_in wA_hi wA_lo wB_in wB_hi wB_lo").split()]

    def load(self, sp, w):
        sp.dma_start(self.wst[:, :, CW:], w[:, CW:].rearrange("(k p) c -> p k c", p=P)).then_inc(self.wB_in, 16)
        sp.dma_start(self.wst[:, :, 0:CW], w[:, 0:CW].rearrange("(k p) c -> p k c", p=P)).then_inc(self.wA_in, 16)

    def sync(self, sp):
        sp.dma_start(self.wdt[:, :, :], self.wdtT.rearrange("(k p) c -> p k c", p=P)).then_inc(self.wdt_in, 16)
        sp.dma_start(self.hp[:, :, :], self.heads_par).then_inc(self.hp_in, 16)
        self.load(sp, self.winG[0])

    def gpsimd(self, pool):
        ident, upto, after, idt = self.ident, self.upto, self.after, self.idt
        identity(pool, ident[:, :], idt)
        pool.memset(upto[:, :], 1.0).then_inc(idt, 1)
        pool.memset(after[:, :], 1.0).then_inc(idt, 1)
        pool.wait_ge(idt, 4)
        pool.affine_select(out=upto[:, :], in_=upto[:, :], compare_op=ALU.is_ge, fill=0.0, base=0,
                           pattern=[[1, P]], channel_multiplier=-1).then_inc(idt, 1)
        pool.affine_select(out=after[:, :], in_=after[:, :], compare_op=ALU.is_ge, fill=0.0, base=-1,
                           pattern=[[-1, P]], channel_multiplier=1).then_inc(idt, 1)
        pool.wait_ge(idt, 6)
        pool.affine_select(out=upto[:, TOK:P], in_=upto[:, TOK:P], compare_op=ALU.is_ge, fill=0.0, base=-TOK,
                           pattern=[[0, TOK]], channel_multiplier=1).then_inc(idt, 1)
        pool.affine_select(out=after[:, 0:TOK], in_=after[:, 0:TOK], compare_op=ALU.is_ge, fill=0.0, base=TOK - 1,
                           pattern=[[0, TOK]], channel_multiplier=-1).then_inc(idt, 1)
        pool.wait_ge(idt, 8)

    def scalar(self, act):
        act.wait_ge(self.wdt_in, 16)
        act.activation(self.wdh[:, :, :], self.wdt[:, :, :], ACT.Copy, scale=S_W).then_inc(self.wdt_hi, 1)
        for c, w_in, w_hi in ((slice(CW, NIN * P), self.wB_in, self.wB_hi), (slice(0, CW), self.wA_in, self.wA_hi)):
            act.wait_ge(w_in, 16)
            act.activation(self.wh[:, :, c], self.wst[:, :, c], ACT.Copy, scale=S_W).then_inc(w_hi, 1)

    def vector(self, dve):
        dve.memset(self.eps[:, :], EPS)
        dve.memset(self.ones[:, :], 1.0).then_inc(self.cst, 1)
        dve.wait_ge(self.wdt_hi, 1)
        dve.scalar_tensor_tensor(out=self.wdl[:, :, :], in0=self.wdt[:, :, :], scalar=S_W, in1=self.wdh[:, :, :],
                                 op0=ALU.mult, op1=ALU.subtract).then_inc(self.wdt_lo, 1)
        for c, w_hi, w_lo in ((slice(CW, NIN * P), self.wB_hi, self.wB_lo), (slice(0, CW), self.wA_hi, self.wA_lo)):
            dve.wait_ge(w_hi, 1)
            dve.scalar_tensor_tensor(out=self.wl[:, :, c], in0=self.wst[:, :, c], scalar=S_W, in1=self.wh[:, :, c],
                                     op0=ALU.mult, op1=ALU.subtract).then_inc(w_lo, 1)


def state_space(nc, start, winG, woutG, params, x1):
    with ExitStack() as ctx:
        def sb(name, shape, dt=F32):
            return ctx.enter_context(nc.sbuf_tensor(name, shape, dt))

        def sem(name):
            return ctx.enter_context(nc.semaphore("m_" + name))

        G = GROUPS
        ident, ones, upto, after, eps, hp = start.ident, start.ones, start.upto, start.after, start.eps, start.hp
        wst, wh, wl, wdh, wdl = start.wst, start.wh, start.wl, start.wdh, start.wdl
        hp_in, wdt_lo = start.hp_in, start.wdt_lo
        wA_in, wA_hi, wA_lo, wB_in, wB_hi, wB_lo = start.wA_in, start.wA_hi, start.wA_lo, start.wB_in, start.wB_hi, start.wB_lo
        th = sb("m_th", [P, KC, ND], F16)
        tl = sb("m_tl", [P, KC, ND], F16)
        wost = sb("m_wost", [P, GCH, HID])
        woh = sb("m_woh", [P, GCH, HID], F16)
        wol = sb("m_wol", [P, GCH, HID], F16)
        par = sb("m_par", [P, 2, NPAR])
        sp_ = [sb(f"m_sp{i}", [P, TT, SSM_HEADS]) for i in range(6)]
        dt = sb("m_dt", [P, TT, SSM_HEADS])
        a = sb("m_a", [P, TT, SSM_HEADS])
        dtg = sb("m_dtg", [P, TT, GH])
        ag = sb("m_ag", [P, TT, GH])
        cv = sb("m_cv", [P, 2, ND])
        xc = sb("m_xc", [P, CONV, ND])
        gate = sb("m_gate", [P, GCH, ND])
        dtx = sb("m_dtx", [P, 2, GH * SSM_P])
        cbm = sb("m_cbm", [P, 2, P])
        R = sb("m_R", [P, 2, 4, P])
        E = sb("m_E", [P, 4, 4, P])
        yt = sb("m_yt", [P, 2, GCH, P])
        y = sb("m_y", [P, GCH, ND])
        sqb = sb("m_sqb", [P, 2, GCH, P])
        sd = sb("m_sd", [P, ND])
        rs = sb("m_rs", [P, ND])
        yh = sb("m_yh", [P, GCH, ND], F16)
        yl = sb("m_yl", [P, GCH, ND], F16)
        bank = [ctx.enter_context(nc.psum_tensor(f"m_b{i}", [P, 512], F32)) for i in range(8)]
        pI, pX, pCB, pD, pY, pO, pS = (bank[0], bank[1], bank[3]), bank[2], bank[3], bank[4], bank[5], bank[6], bank[7]

        (dtp, sp_dve, sp_act, dt_ok, wC_in, wC_hi, wC_lo, ip, cv0, cvs, conv, silu, gat, agc, xt, dx, cb, cm, r_ok, d_ok,
         e_ok, m_ok, y_ok, yev, sqy, ssm, sdy, rsy, yn, yg, yhi, ylo, op, acc) = [sem(n) for n in (
             "dtp sp_dve sp_act dt_ok wC_in wC_hi wC_lo ip cv0 cvs conv silu gat agc xt dx cb cm r_ok d_ok "
             "e_ok m_ok y_ok yev sqy ssm sdy rsy yn yg yhi ylo op acc").split()]
        par_in = sem("par_in")
        taps = sem("taps")
        ln = LayerNorm(nc, ctx, "mln", x1, ident[:, :], eps[:, 0:1], pI[0:2], (th, tl))
        block = ctx.enter_context(nc.Block())

        def loop(eng, body):
            body(0)
            with eng.Fori(1, G - 1) as g:
                body(g)
            body(G - 1)

        def at_last(g):
            return isinstance(g, int) and g == G - 1

        def at_first(g):
            return isinstance(g, int) and g == 0

        @block.sync
        def _(sp):
            def body(g):
                w, w_out = row(winG, g), row(woutG, g)
                if not at_first(g):
                    wait(sp, wA_lo, g)
                    start.load(sp, w)
                wait(sp, wC_lo, g)
                sp.dma_start(wost[:, :, :], w_out.rearrange("(k p) c -> p k c", p=P)).then_inc(wC_in, 16)
            loop(sp, body)

        @block.gpsimd
        def _(pool):
            def normalise(g):
                wait(pool, rsy, g + 1)
                for j in range(GCH):
                    pool.tensor_tensor(y[:, j, :], y[:, j, :], rs[:, :], ALU.mult).then_inc(yn, 1)

            def body(g):
                wait(pool, yg, TT * g)
                pool.dma_start(par[:, 0, :], row(params, g)).then_inc(par_in, 16)
                if not at_first(g):
                    normalise(g - 1)
                for t in range(TT):
                    for q in range(2):
                        n = 8 * g + 2 * t + q
                        wait(pool, agc, 2 * (g + 1))
                        wait(pool, d_ok, n - 1)
                        pool.tensor_tensor(R[:, q, :, :], upto[:, :].unsqueeze(1).to_broadcast([P, 4, P]),
                                           ag[:, t, 4 * q:4 * q + 4].unsqueeze(2).to_broadcast([P, 4, P]), ALU.mult).then_inc(r_ok, 1)
            loop(pool, body)
            pool.wait_ge(yg, TT * G)
            normalise(G - 1)

        @block.tensor
        def _(pe):
            ln.tensor(pe)
            pe.wait_ge(ln.done, TT)
            pe.wait_ge(wdt_lo, 1)
            for t in range(TT):
                for k in range(KC):
                    mm = split3(pe, pD[:, t * SSM_HEADS:(t + 1) * SSM_HEADS], (th[:, k, t * P:(t + 1) * P], tl[:, k, t * P:(t + 1) * P]),
                                (wdh[:, k, :], wdl[:, k, :]), k == 0, k == KC - 1)
            mm.then_inc(dtp, 1)

            def input_chunk(g, n):
                wait(pe, wB_lo if n < GCH else wA_lo, g + 1)
                if n >= 3 + GCH:
                    wait(pe, conv, CONV * g + n - GCH - 2)
                elif n >= 3:
                    wait(pe, gat, GCH * g + n - 2)
                c = (CONV + n if n < GCH else n - GCH) * P
                for k in range(KC):
                    mm = split3(pe, pI[n % 3][:, :], (wh[:, k, c:c + P], wl[:, k, c:c + P]),
                                (th[:, k, :], tl[:, k, :]), k == 0, k == KC - 1)
                mm.then_inc(ip, 1)

            def out_tile(g, t):
                wait(pe, ylo, GCH * (g + 1))
                wait(pe, wC_lo, g + 1)
                wait(pe, acc, TT * (g + 1) + t)
                for j in range(GCH):
                    mm = split3(pe, pO[:, :], (yh[:, j, t * P:(t + 1) * P], yl[:, j, t * P:(t + 1) * P]),
                                (woh[:, j, :], wol[:, j, :]), j == 0, j == GCH - 1)
                mm.then_inc(op, 1)

            def decay(g, t, q):
                n = 8 * g + 2 * t + q
                wait(pe, r_ok, n + 1)
                wait(pe, e_ok, n)
                if at_first(g) and n == 0:
                    pe.wait_ge(dt_ok, 1)
                pe.matmul(pD[:, :], after[:, :], R[:, q, :, :], start=True, stop=True).then_inc(d_ok, 1)

            def outputs(g, t):
                wait(pe, m_ok, 8 * g + 2 * t + 2)
                wait(pe, dx, TT * g + t + 1)
                wait(pe, yev, TT * g + t)
                for h in range(GH):
                    mm = pe.matmul(pY[64 * (h % 2):64 * (h % 2) + 64, (h // 2) * P:(h // 2) * P + P],
                                   dtx[:, t % 2, h * SSM_P:(h + 1) * SSM_P], E[:, 2 * (t % 2) + h // 4, h % 4, :],
                                   start=True, stop=True)
                mm.then_inc(y_ok, 1)

            def turn_x(g, t):
                cols = slice(t * P, (t + 1) * P)
                wait(pe, silu, CONV * (g + 1))
                wait(pe, dx, TT * g + t)
                for j in range(GCH):
                    mm = pe.transpose(pX[:, j * P:(j + 1) * P], xc[:, j, cols], ident[:, :])
                mm.then_inc(xt, 1)
                wait(pe, cm, TT * g + t)
                pe.matmul(pCB[:, 0:P], xc[:, GCH, cols], xc[:, GCH + 1, cols], start=True, stop=True).then_inc(cb, 1)

            def squares(g, t):
                if t == 0:
                    wait(pe, sdy, g)
                wait(pe, sqy, TT * g + t + 1)
                for j in range(GCH):
                    mm = pe.matmul(pS[:, t * P:(t + 1) * P], ones[:, :], sqb[:, t % 2, j, :], start=j == 0, stop=j == GCH - 1)
                mm.then_inc(ssm, 1)

            def body(g):
                input_chunk(g, 0)
                if not at_first(g):
                    squares(g - 1, TT - 2)
                input_chunk(g, 1)
                if not at_first(g):
                    squares(g - 1, TT - 1)
                for n in range(2, NIN):
                    input_chunk(g, n)
                for t in range(TT):
                    if t:
                        turn_x(g, t)
                    decay(g, t, 0)
                    if t == TT - 1:
                        outputs(g, t - 1)
                    if t == 0:
                        if not at_first(g):
                            out_tile(g - 1, 0)
                        turn_x(g, t)
                    if t < 2 and not at_first(g):
                        out_tile(g - 1, t + 1)
                    if t >= 2:
                        squares(g, t - 2)
                    decay(g, t, 1)
                    if 0 < t < TT - 1:
                        outputs(g, t - 1)
                if not at_first(g):
                    out_tile(g - 1, TT - 1)
                outputs(g, TT - 1)
            loop(pe, body)
            squares(G - 1, TT - 2)
            squares(G - 1, TT - 1)
            for t in range(TT):
                out_tile(G - 1, t)

        @block.scalar
        def _(act):
            ln.scalar(act)
            ln.scalar_turned(act)

            def split(g, part):
                if part == "A":
                    wait(act, wA_in, 16 * (g + 1))
                    wait(act, ip, NIN * g)
                    c = slice(0, CW)
                    act.activation(wh[:, :, c], wst[:, :, c], ACT.Copy, scale=S_W).then_inc(wA_hi, 1)
                elif part == "B":
                    wait(act, wB_in, 16 * (g + 1))
                    wait(act, ip, NIN * g)
                    c = slice(CW, NIN * P)
                    act.activation(wh[:, :, c], wst[:, :, c], ACT.Copy, scale=S_W).then_inc(wB_hi, 1)
                else:
                    wait(act, wC_in, 16 * (g + 1))
                    wait(act, acc, TT * (g + 1))
                    act.activation(woh[:, :, :], wost[:, :, :], ACT.Copy, scale=S_W).then_inc(wC_hi, 1)

            act.wait_ge(sp_dve, 2)
            act.activation(sp_[2][:, :, :], sp_[1][:, :, :], ACT.Exp).then_inc(sp_act, 1)
            act.wait_ge(hp_in, 16)
            act.activation(hp[:, 1, :], hp[:, 1, :], ACT.Exp).then_inc(sp_act, 1)
            act.wait_ge(sp_dve, 3)
            act.activation(sp_[4][:, :, :], sp_[3][:, :, :], ACT.Ln).then_inc(sp_act, 1)

            def finish_conv(g, j):
                wait(act, conv, CONV * g + j + 1)
                if j == 0:
                    wait(act, yev, TT * g)
                act.activation(xc[:, j, :], cv[:, j % 2, :], ACT.Silu).then_inc(silu, 1)

            def square(g, t):
                wait(act, yev, TT * g + t + 1)
                wait(act, ssm, TT * g + t - 1)
                act.activation(sqb[:, t % 2, :, :], yt[:, t % 2, :, :], ACT.Square).then_inc(sqy, 1)

            def close(g):
                square(g, TT - 2)
                square(g, TT - 1)
                split(g, "C")
                wait(act, ssm, TT * (g + 1))
                act.activation(sd[:, :], pS[:, :], ACT.Sqrt, bias=eps[:, 0:1], scale=1.0 / (GCH * P)).then_inc(sdy, 1)

            def high(g, j):
                wait(act, yn, GCH * g + j + 1)
                act.activation(yh[:, j, :], y[:, j, :], ACT.Copy, scale=S_Y).then_inc(yhi, 1)

            def body(g):
                if not at_first(g):
                    close(g - 1)
                for j in range(GCH):
                    wait(act, ip, NIN * g + j + 1)
                    if j == 0:
                        wait(act, yg, TT * g)
                    act.activation(gate[:, j, :], pI[j % 3][:, :], ACT.Silu, scale=1.0 / (S_H * S_W)).then_inc(gat, 1)
                if not at_first(g):
                    high(g - 1, 0)
                    high(g - 1, 1)
                wait(act, taps, g + 1)
                for j in range(CONV):
                    wait(act, ip, NIN * g + GCH + j + 1)
                    wait(act, silu, CONV * g + j - 1)
                    act.activation(cv[:, j % 2, :], pI[(GCH + j) % 3][:, :], ACT.Identity,
                                   bias=par[:, 0, CONV * TAPS + j:CONV * TAPS + j + 1],
                                   scale=par[:, 1, j * TAPS + TAPS - 1:j * TAPS + TAPS]).then_inc(cv0, 1)
                    if j + 2 < GCH and not at_first(g):
                        high(g - 1, j + 2)
                    if j:
                        finish_conv(g, j - 1)
                finish_conv(g, CONV - 1)
                for t in range(TT):
                    for q in range(2):
                        n = 8 * g + 2 * t + q
                        wait(act, d_ok, n + 1)
                        wait(act, y_ok, TT * g + t - 1)
                        act.activation(E[:, 2 * (t % 2) + q, :, :], pD[:, :].rearrange("p (h c) -> p h c", h=4), ACT.Exp).then_inc(e_ok, 1)
                        if q == 0 and t >= 2:
                            square(g, t - 2)
                    if t in (1, 2) and not at_last(g):
                        split(g + 1, "B" if t == 1 else "A")
            loop(act, body)
            close(G - 1)
            for j in range(GCH):
                high(G - 1, j)

        @block.vector
        def _(dve):
            ln.vector(dve)
            ln.vector_turned(dve)
            dve.sem_inc(acc, TT)

            def split(g, part):
                if part == "A":
                    wait(dve, wA_hi, g + 1)
                    c = slice(0, CW)
                    dve.scalar_tensor_tensor(out=wl[:, :, c], in0=wst[:, :, c], scalar=S_W, in1=wh[:, :, c],
                                             op0=ALU.mult, op1=ALU.subtract).then_inc(wA_lo, 1)
                elif part == "B":
                    wait(dve, wB_hi, g + 1)
                    c = slice(CW, NIN * P)
                    dve.scalar_tensor_tensor(out=wl[:, :, c], in0=wst[:, :, c], scalar=S_W, in1=wh[:, :, c],
                                             op0=ALU.mult, op1=ALU.subtract).then_inc(wB_lo, 1)
                else:
                    wait(dve, wC_hi, g + 1)
                    dve.scalar_tensor_tensor(out=wol[:, :, :], in0=wost[:, :, :], scalar=S_W, in1=woh[:, :, :],
                                             op0=ALU.mult, op1=ALU.subtract).then_inc(wC_lo, 1)

            v, nv, e, u1, lnu, tmp = [x_[:, :, :] for x_ in sp_]
            step = [0]

            def link(ins):
                step[0] += 1
                ins.then_inc(sp_dve, 1)
                dve.wait_ge(sp_dve, step[0])

            dve.wait_ge(dtp, 1)
            dve.wait_ge(hp_in, 16)
            link(dve.scalar_tensor_tensor(out=v, in0=pD[:, 0:TT * SSM_HEADS].rearrange("p (t h) -> p t h", t=TT), scalar=1.0 / (S_H * S_W),
                                          in1=hp[:, 0, :].unsqueeze(1).to_broadcast([P, TT, SSM_HEADS]), op0=ALU.mult, op1=ALU.add))
            link(dve.scalar_tensor_tensor(out=nv, in0=v, scalar=-1.0, in1=v, op0=ALU.mult, op1=ALU.min))
            dve.wait_ge(sp_act, 2)
            link(dve.tensor_scalar(u1, e, 1.0, None, ALU.add))
            dve.wait_ge(sp_act, 3)
            link(dve.tensor_scalar(u1, u1, 1.0, None, ALU.subtract))
            link(dve.tensor_scalar(tmp, u1, 0.0, None, ALU.is_equal))
            link(dve.tensor_tensor(lnu, lnu, tmp, ALU.add))
            link(dve.tensor_tensor(u1, u1, tmp, ALU.add))
            link(dve.reciprocal(tmp, u1))
            link(dve.tensor_tensor(tmp, tmp, lnu, ALU.mult))
            link(dve.tensor_tensor(tmp, tmp, e, ALU.mult))
            link(dve.scalar_tensor_tensor(out=dt[:, :, :], in0=v, scalar=0.0, in1=tmp, op0=ALU.max, op1=ALU.add))
            link(dve.tensor_tensor(a[:, :, :], dt[:, :, :], hp[:, 1, :].unsqueeze(1).to_broadcast([P, TT, SSM_HEADS]), ALU.mult))
            link(dve.tensor_scalar(a[:, :, :], a[:, :, :], -1.0, -1.0e4, ALU.mult, ALU.max))
            dve.nop().then_inc(dt_ok, 1)

            def y_out(g, t):
                wait(dve, y_ok, TT * g + t + 1)
                wait(dve, sqy, TT * g + t - 1)
                wait(dve, yg, TT * g + t - 1)
                cols = slice(t * P, (t + 1) * P)
                for j in range(GCH):
                    d = par[:, 0, CONV * TAPS + CONV + j:CONV * TAPS + CONV + j + 1]
                    i = dve.scalar_tensor_tensor(out=yt[:, t % 2, j, :], in0=xc[:, j, cols], scalar=d, in1=pY[:, j * P:(j + 1) * P],
                                                 op0=ALU.mult, op1=ALU.add)
                i.then_inc(yev, 1)
                wait(dve, yev, TT * g + t + 1)
                wait(dve, gat, GCH * (g + 1))
                if t == 0:
                    wait(dve, yhi, GCH * g)
                    wait(dve, ylo, GCH * g)
                for j in range(GCH):
                    nw = par[:, 0, CONV * TAPS + CONV + GCH + j:CONV * TAPS + CONV + GCH + j + 1]
                    i = dve.scalar_tensor_tensor(out=y[:, j, cols], in0=yt[:, t % 2, j, :], scalar=nw, in1=gate[:, j, cols],
                                                 op0=ALU.mult, op1=ALU.mult)
                i.then_inc(yg, 1)

            def accumulate(g, t):
                wait(dve, op, TT * g + t + 1)
                wait(dve, acc, TT * g + t + 1)
                dve.scalar_tensor_tensor(out=x1[:, t, :], in0=pO[:, :], scalar=1.0 / (S_Y * S_W), in1=x1[:, t, :],
                                         op0=ALU.mult, op1=ALU.add).then_inc(acc, 1)

            def masked(g, t, q):
                wait(dve, e_ok, 8 * g + 2 * t + q + 1)
                wait(dve, cm, TT * g + t + 1)
                Eb = E[:, 2 * (t % 2) + q, :, :]
                dve.tensor_tensor(Eb, Eb, cbm[:, t % 2, :].unsqueeze(1).to_broadcast([P, 4, P]), ALU.mult).then_inc(m_ok, 1)

            def close(g):
                wait(dve, sdy, g + 1)
                dve.reciprocal(rs[:, :], sd[:, :]).then_inc(rsy, 1)
                split(g, "C")

            def low(g, j):
                wait(dve, yhi, GCH * g + j + 1)
                dve.scalar_tensor_tensor(out=yl[:, j, :], in0=y[:, j, :], scalar=S_Y, in1=yh[:, j, :],
                                         op0=ALU.mult, op1=ALU.subtract).then_inc(ylo, 1)

            def body(g):
                hd = slice(GH * g, GH * g + GH) if isinstance(g, int) else bass.ds(g * GH, GH)
                wait(dve, r_ok, 8 * g)
                dve.tensor_copy(ag[:, :, :], a[:, :, hd]).then_inc(agc, 1)
                wait(dve, dx, TT * g)
                dve.tensor_copy(dtg[:, :, :], dt[:, :, hd]).then_inc(agc, 1)
                wait(dve, par_in, 16 * (g + 1))
                dve.tensor_scalar(par[:, 1, 0:CONV * TAPS], par[:, 0, 0:CONV * TAPS], 1.0 / (S_H * S_W), None, ALU.mult).then_inc(taps, 1)
                if not at_first(g):
                    split(g, "A")
                    close(g - 1)
                    low(g - 1, 0)
                    low(g - 1, 1)
                wait(dve, taps, g + 1)
                for j in range(CONV):
                    n = CONV * g + j
                    wait(dve, cv0, n + 1)
                    acc_v = cv[:, j % 2, :].rearrange("p (b q) -> p b q", b=BATCH)
                    src = pI[(GCH + j) % 3][:, :].rearrange("p (b q) -> p b q", b=BATCH)
                    for m in range(1, TAPS):
                        if m > 1:
                            wait(dve, cvs, 2 * n + m - 1)
                        tap = par[:, 1, j * TAPS + TAPS - 1 - m:j * TAPS + TAPS - m]
                        i = dve.scalar_tensor_tensor(out=acc_v[:, :, m:], in0=src[:, :, 0:TOK - m], scalar=tap, in1=acc_v[:, :, m:],
                                                     op0=ALU.mult, op1=ALU.add)
                        i.then_inc(cvs if m < TAPS - 1 else conv, 1)
                    if j + 2 < GCH and not at_first(g):
                        low(g - 1, j + 2)
                wait(dve, agc, 2 * (g + 1))
                for t in range(TT):
                    if t == 0 and not at_first(g):
                        accumulate(g - 1, t)
                    wait(dve, xt, TT * g + t + 1)
                    wait(dve, y_ok, TT * g + t - 1)
                    dve.tensor_tensor(dtx[:, t % 2, :].rearrange("p (h c) -> p h c", h=GH), pX[:, :].rearrange("p (h c) -> p h c", h=GH),
                                      dtg[:, t, :].unsqueeze(2).to_broadcast([P, GH, SSM_P]), ALU.mult).then_inc(dx, 1)
                    wait(dve, cb, TT * g + t + 1)
                    wait(dve, m_ok, 8 * g + 2 * t - 2)
                    dve.tensor_tensor(cbm[:, t % 2, :], pCB[:, 0:P], upto[:, :], ALU.mult).then_inc(cm, 1)
                    masked(g, t, 0)
                    if t < 2 and not at_first(g):
                        accumulate(g - 1, t + 1)
                    if t == TT - 1:
                        y_out(g, t - 1)
                    masked(g, t, 1)
                    if 0 < t < TT - 1:
                        y_out(g, t - 1)
                    if t == 1 and not at_last(g):
                        split(g + 1, "B")
                if not at_first(g):
                    accumulate(g - 1, TT - 1)
                y_out(g, TT - 1)
            loop(dve, body)
            close(G - 1)
            for j in range(GCH):
                low(G - 1, j)
            for t in range(TT):
                accumulate(G - 1, t)


def experts(nc, start, raT, bwT, out, x2):
    with ExitStack() as ctx:
        def sb(name, shape, dt=F32):
            return ctx.enter_context(nc.sbuf_tensor("f_" + name, shape, dt))

        def sem(name):
            return ctx.enter_context(nc.semaphore("f_" + name))

        N = EXPERTS + EXPERTS * RANK
        ident, eps = start.ident, start.eps
        hT = sb("hT", [P, KC, ND])
        ra = sb("ra", [P, KC, N])
        bw = sb("bw", [P, HID])
        lg = sb("lg", [P, TT, N])
        top = sb("top", [P, TT])
        eq = sb("eq", [P, TT, EXPERTS])
        pr = sb("pr", [P, TT, EXPERTS])
        rank = sb("rank", [P, EXPERTS])
        best = sb("best", [P, TT])
        wt = sb("wt", [P, TT, EXPERTS])
        wh = sb("wh", [P, TT, P])
        whT = sb("whT", [P, TT, P])
        bank = [ctx.enter_context(nc.psum_tensor(f"f_b{i}", [P, 512], F32)) for i in range(8)]
        w_in, cst, lgp, chain, whp, wht, outp, added, stored = [
            sem(n) for n in "w_in cst lgp chain whp wht outp added stored".split()]
        ln = LayerNorm(nc, ctx, "fln", x2, ident[:, :], eps[:, 0:1], bank[0:2], (hT,))
        block = ctx.enter_context(nc.Block())

        @block.sync
        def _(sp):
            sp.dma_start(ra[:, :, :], raT.rearrange("(k p) c -> p k c", p=P)).then_inc(w_in, 16)
            sp.dma_start(bw[:, :], bwT).then_inc(w_in, 16)
            sp.wait_ge(added, TT)
            sp.dma_start(out.rearrange("(t p) c -> p t c", p=P), x2[:, :, :]).then_inc(stored, 16)
            sp.wait_ge(stored, 16)

        @block.scalar
        def _(act):
            ln.scalar(act)
            ln.scalar_turned(act)

        @block.tensor
        def _(pe):
            ln.tensor(pe)
            pe.wait_ge(ln.done, TT)
            pe.wait_ge(w_in, 32)
            for t in range(TT):
                for k in range(KC):
                    mm = pe.matmul(bank[2 + t // 2][:, (t % 2) * 256:(t % 2) * 256 + N], hT[:, k, t * P:(t + 1) * P], ra[:, k, :],
                                   start=k == 0, stop=k == KC - 1)
            mm.then_inc(lgp, 1)
            pe.wait_ge(whp, 1)
            for t in range(TT):
                mm = pe.transpose(bank[0][:, t * P:(t + 1) * P], wh[:, t, :], ident[:, :])
            mm.then_inc(wht, 1)
            pe.wait_ge(whp, 2)
            for t in range(TT):
                pe.matmul(bank[4 + t][:, :], whT[:, t, :], bw[:, :], start=True, stop=True).then_inc(outp, 1)

        @block.vector
        def _(dve):
            for e in range(EXPERTS):
                i = dve.memset(rank[:, e:e + 1], float(EXPERTS - e))
            i.then_inc(cst, 1)
            ln.vector(dve)
            ln.vector_turned(dve)
            dve.wait_ge(cst, 1)
            step = [0]

            def link(ins):
                step[0] += 1
                ins.then_inc(chain, 1)
                dve.wait_ge(chain, step[0])

            dve.wait_ge(lgp, 1)
            for i in range(2):
                link(dve.tensor_copy(lg[:, 2 * i:2 * i + 2, :], bank[2 + i][:, :].rearrange("p (t c) -> p t c", t=2)[:, :, 0:N]))
            logits = lg[:, :, 0:EXPERTS]
            link(dve.tensor_reduce(top[:, :], logits, AX.X, ALU.max))
            topb = top[:, :].unsqueeze(2).to_broadcast([P, TT, EXPERTS])
            link(dve.tensor_tensor(eq[:, :, :], logits, topb, ALU.is_equal))
            link(dve.tensor_tensor(pr[:, :, :], eq[:, :, :], rank[:, :].unsqueeze(1).to_broadcast([P, TT, EXPERTS]), ALU.mult))
            link(dve.tensor_reduce(best[:, :], pr[:, :, :], AX.X, ALU.max))
            link(dve.tensor_tensor(eq[:, :, :], pr[:, :, :], best[:, :].unsqueeze(2).to_broadcast([P, TT, EXPERTS]), ALU.is_equal))
            link(dve.tensor_tensor(wt[:, :, :], eq[:, :, :], topb, ALU.mult))
            for t in range(TT):
                i = dve.tensor_tensor(wh[:, t, :].rearrange("p (e r) -> p e r", e=EXPERTS),
                                      lg[:, t, EXPERTS:N].rearrange("p (e r) -> p e r", e=EXPERTS),
                                      wt[:, t, :].unsqueeze(2).to_broadcast([P, EXPERTS, RANK]), ALU.mult)
            i.then_inc(whp, 1)
            dve.wait_ge(wht, 1)
            dve.tensor_copy(whT[:, :, :], bank[0][:, :].rearrange("p (t c) -> p t c", t=TT)).then_inc(whp, 1)
            for t in range(TT):
                dve.wait_ge(outp, t + 1)
                dve.tensor_tensor(x2[:, t, :], bank[4 + t][:, :], x2[:, t, :], ALU.add).then_inc(added, 1)


def perceiver_block(nc, x, ctxT, maskT, wqT, wkT, wvT, woT, norm_w, winG, wdtT, woutG, params, heads_par, raT, bwT, out):
    q_hi = nc.dram_tensor("q_hi_scratch", [BATCH, P, HEADS * TOK], F16, kind="Internal").ap()
    q_lo = nc.dram_tensor("q_lo_scratch", [BATCH, P, HEADS * TOK], F16, kind="Internal").ap()
    o_dram = nc.dram_tensor("o_scratch", [BATCH, P, HEADS * TOK], F32, kind="Internal").ap()
    with ExitStack() as ctx:
        ctx_parts = [ctx.enter_context(nc.sbuf_tensor(n, [P, KC, KEYS + pad], dt))
                     for n, dt, pad in (("ctx_f", F32, 0), ("ctx_h", F16, 3), ("ctx_l", F16, 3))]
        kv_parts = [ctx.enter_context(nc.sbuf_tensor(n, [P, 2, KC, KV_HEADS * HD], F16)) for n in ("w_h", "w_l")]
        q_stored = [ctx.enter_context(nc.semaphore(f"q_stored{i}")) for i in range(3)]
        queries(nc, x, wqT, norm_w, q_hi, q_lo, (wkT, wvT), ctxT, kv_parts, ctx_parts, q_stored)
        cross_attention(nc, ctxT, maskT, kv_parts, ctx_parts, q_hi, q_lo, q_stored, o_dram)
    with ExitStack() as ctx:
        x1 = ctx.enter_context(nc.sbuf_tensor("x1", [P, TT, HID], F32))
        start = SsmStart(nc, ctx, winG, wdtT, heads_par)
        output_projection(nc, start, x, woT, o_dram, x1)
        state_space(nc, start, winG, woutG, params, x1)
        experts(nc, start, raT, bwT, out, x1)


def kernel(**inputs):
    import numpy as np
    import concourse.bacc as bacc
    from concourse.bass_utils import run_bass_kernel_spmd

    a = {n: np.asarray(v) for n, v in inputs.items()}
    win = a["L0_attn_in_proj_w"].T
    conv_dim = INNER + 2 * GROUPS * P

    def group_columns(g):
        gw = GCH * P
        return [win[:, INNER + g * gw:INNER + (g + 1) * gw],
                win[:, 2 * INNER + g * P:2 * INNER + (g + 1) * P],
                win[:, 2 * INNER + GROUPS * P + g * P:2 * INNER + GROUPS * P + (g + 1) * P],
                win[:, g * gw:(g + 1) * gw]]

    def conv_rows(v, g):
        gw = GCH * P
        rows = np.concatenate([v[g * gw:(g + 1) * gw], v[INNER + g * P:INNER + (g + 1) * P],
                               v[INNER + GROUPS * P + g * P:INNER + GROUPS * P + (g + 1) * P]])
        return rows.reshape((CONV, P) + v.shape[1:]).swapaxes(0, 1)

    def channels(v, g):
        return v[g * GCH * P:(g + 1) * GCH * P].reshape(GCH, P).T

    d_rows = np.repeat(a["L0_attn_D"], SSM_P)
    params = np.stack([np.concatenate([conv_rows(a["L0_attn_conv_weight"], g).reshape(P, CONV * TAPS),
                                       conv_rows(a["L0_attn_conv_bias"], g), channels(d_rows, g),
                                       channels(a["L0_attn_norm_weight"], g)], axis=1) for g in range(GROUPS)])
    data = {
        "x": a["x"].reshape(ND, HID),
        "ctxT": a["ctx_4096"].transpose(0, 2, 1),
        "maskT": a["mask_1x1xSxS2_ff0"].reshape(TOK, KEYS).T,
        "wqT": a["L0_xattn_q_proj_w"].T,
        "wkT": a["L0_xattn_k_proj_w"].T,
        "wvT": a["L0_xattn_v_proj_w"].T,
        "woT": a["L0_xattn_o_proj_w"].T,
        "norm_w": np.stack([a["L0_xattn_q_norm_w"], a["L0_xattn_k_norm_w"]], axis=1),
        "winG": np.stack([np.concatenate(group_columns(g), axis=1) for g in range(GROUPS)]),
        "wdtT": win[:, INNER + conv_dim:],
        "woutG": a["L0_attn_out_proj_w"].T.reshape(GROUPS, GCH * P, HID),
        "params": params,
        "heads_par": np.ascontiguousarray(np.broadcast_to(np.stack([a["L0_attn_dt_bias"], a["L0_attn_A_log"]]), (P, 2, SSM_HEADS))),
        "raT": np.concatenate([a["L0_ffn_route_w"], a["L0_ffn_A"].reshape(EXPERTS * RANK, HID)]).T,
        "bwT": a["L0_ffn_Bw"].transpose(0, 2, 1).reshape(EXPERTS * RANK, HID),
    }
    nc = bacc.Bacc("TRN2", target_bir_lowering=False, num_devices=1)
    arrays, args = {}, {}
    for name, v in data.items():
        arrays[name + "_dram"] = np.ascontiguousarray(v)
        args[name] = nc.dram_tensor(name + "_dram", v.shape, F32, kind="ExternalInput").ap()
    out = nc.dram_tensor("out_dram", (ND, HID), F32, kind="ExternalOutput").ap()
    perceiver_block(nc, out=out, **args)
    r = run_bass_kernel_spmd(nc, [arrays], core_ids=[0])
    return r.results[0]["out_dram"].reshape(BATCH, TOK, HID)
```
